# Optimizing a Trainium2 kernel written in Bass

```python
import numpy as np
import jax
import jax.numpy as jnp

def _softmax(x, axis=-1):
    return jax.nn.softmax(x, axis=axis)

def _gelu(x):
    return jax.nn.gelu(x, approximate=True)

def _silu(x):
    return jax.nn.silu(x)

def _sigmoid(x):
    return jax.nn.sigmoid(x)

def _layernorm(x, axis=-1, eps=1e-05):
    m = jnp.mean(x, axis=axis, keepdims=True)
    v = jnp.var(x, axis=axis, keepdims=True)
    return (x - m) / jnp.sqrt(v + eps)

def _scatter_add(tgt, idx, src, axis=0):
    return tgt.at[idx].add(src)

def _segment_sum(src, seg, n):
    return jax.ops.segment_sum(src, seg, n)
kernel_name = 'mk_gnn_preln_d1_gnn_r8_733625'

def setup_inputs(seed: int=0):
    np.random.seed(seed)
    _w = jnp.asarray

    def _rec_inputs():
        import jax
        import jax.numpy as jnp
        _gk = jax.random.key(seed)
        x = -0.0005963 + 1.001 * jax.random.normal(jax.random.fold_in(_gk, 1), (384, 1024), jnp.float32)
        _s = jax.random.randint(jax.random.fold_in(_gk, 2), (3072,), 0, 384, jnp.int32)
        _d = jax.random.randint(jax.random.fold_in(_gk, 3), (3072,), 0, 384, jnp.int32)
        _loop = jnp.arange(384, dtype=jnp.int32)
        src = jnp.concatenate([_s, _d, _loop])
        dst = jnp.concatenate([_d, _s, _loop])
        _o = jnp.argsort(dst, stable=True)
        src = src[_o]
        dst = dst[_o]
        edge_type_5 = jax.random.randint(jax.random.fold_in(_gk, 12), (6528,), 0, 5, jnp.int32)
        return (x, src, dst, edge_type_5)
    x, src, dst, edge_type_5 = _rec_inputs()

    def _L0_gnn_setup():
        import jax, jax.numpy as jnp
        import numpy as np
        N = 384
        E = 12288
        IN_F = 1024
        OUT_F = 1024
        H = 16
        D = OUT_F // H
        NUM_ETYPES = 4

        def _build_mask(edge_index, edge_type, edge_type_weights, dtype):
            src, dst = (edge_index[0], edge_index[1])
            w = jax.nn.softplus(edge_type_weights)
            mask = jnp.full((N, N), -jnp.inf, dtype=dtype)
            mask = mask.at[src, dst].set(w[edge_type - 1])
            diag = jnp.diagonal(mask)
            idx = jnp.arange(N)
            mask = mask.at[idx, idx].set(jnp.where(jnp.isneginf(diag), w[3], diag))
            return mask
        key = jax.random.key(seed)
        ks = jax.random.split(key, 20)
        p = lambda k, shape: jax.random.normal(k, shape, dtype=jnp.float32) * 0.02
        return {'x': jax.random.normal(ks[0], (N, IN_F), dtype=jnp.float32), 'edge_index': jax.random.randint(ks[1], (2, E), 0, N), 'edge_type': jax.random.randint(ks[2], (E,), 1, NUM_ETYPES + 1), 'edge_type_weights': jnp.ones((NUM_ETYPES,), jnp.float32) + 0.1 * jax.random.normal(ks[3], (NUM_ETYPES,), dtype=jnp.float32), 'wq': p(ks[4], (OUT_F, IN_F)), 'bq': p(ks[5], (OUT_F,)), 'wk': p(ks[6], (OUT_F, IN_F)), 'bk': p(ks[7], (OUT_F,)), 'wv': p(ks[8], (OUT_F, IN_F)), 'bv': p(ks[9], (OUT_F,)), 'wiq': p(ks[10], (OUT_F, OUT_F)), 'biq': p(ks[11], (OUT_F,)), 'wik': p(ks[12], (OUT_F, OUT_F)), 'bik': p(ks[13], (OUT_F,)), 'wiv': p(ks[14], (OUT_F, OUT_F)), 'biv': p(ks[15], (OUT_F,)), 'wo': p(ks[16], (OUT_F, OUT_F)), 'bo': p(ks[17], (OUT_F,))}
    _L0_gnn_all = _L0_gnn_setup()
    _L0_gnn_in = {k: v for k, v in _L0_gnn_all.items() if k in ('edge_type_weights', 'wq', 'bq', 'wk', 'bk', 'wv', 'bv', 'wiq', 'biq', 'wik', 'bik', 'wiv', 'biv', 'wo', 'bo')}
    del _L0_gnn_all
    return {'x': x, 'src': src, 'dst': dst, 'edge_type_5': edge_type_5, 'L0_gnn_edge_type_weights': _L0_gnn_in['edge_type_weights'], 'L0_gnn_wq': _L0_gnn_in['wq'], 'L0_gnn_bq': _L0_gnn_in['bq'], 'L0_gnn_wk': _L0_gnn_in['wk'], 'L0_gnn_bk': _L0_gnn_in['bk'], 'L0_gnn_wv': _L0_gnn_in['wv'], 'L0_gnn_bv': _L0_gnn_in['bv'], 'L0_gnn_wiq': _L0_gnn_in['wiq'], 'L0_gnn_biq': _L0_gnn_in['biq'], 'L0_gnn_wik': _L0_gnn_in['wik'], 'L0_gnn_bik': _L0_gnn_in['bik'], 'L0_gnn_wiv': _L0_gnn_in['wiv'], 'L0_gnn_biv': _L0_gnn_in['biv'], 'L0_gnn_wo': _L0_gnn_in['wo'], 'L0_gnn_bo': _L0_gnn_in['bo']}

def reference(x, src, dst, edge_type_5, L0_gnn_edge_type_weights, L0_gnn_wq, L0_gnn_bq, L0_gnn_wk, L0_gnn_bk, L0_gnn_wv, L0_gnn_bv, L0_gnn_wiq, L0_gnn_biq, L0_gnn_wik, L0_gnn_bik, L0_gnn_wiv, L0_gnn_biv, L0_gnn_wo, L0_gnn_bo):
    import jax
    import jax.numpy as jnp

    def _L0_gnn_ref(x, edge_index, edge_type, edge_type_weights, wq, bq, wk, bk, wv, bv, wiq, biq, wik, bik, wiv, biv, wo, bo):
        import jax, jax.numpy as jnp
        import numpy as np
        N = 384
        E = 12288
        IN_F = 1024
        OUT_F = 1024
        H = 16
        D = OUT_F // H
        NUM_ETYPES = 4

        def _build_mask(edge_index, edge_type, edge_type_weights, dtype):
            src, dst = (edge_index[0], edge_index[1])
            w = jax.nn.softplus(edge_type_weights)
            mask = jnp.full((N, N), -jnp.inf, dtype=dtype)
            mask = mask.at[src, dst].set(w[edge_type - 1])
            diag = jnp.diagonal(mask)
            idx = jnp.arange(N)
            mask = mask.at[idx, idx].set(jnp.where(jnp.isneginf(diag), w[3], diag))
            return mask
        q = x @ wq.T + bq
        k = x @ wk.T + bk
        v = x @ wv.T + bv
        q2 = (q @ wiq.T + biq).reshape(N, H, D).transpose(1, 0, 2)
        k2 = (k @ wik.T + bik).reshape(N, H, D).transpose(1, 0, 2)
        v2 = (v @ wiv.T + biv).reshape(N, H, D).transpose(1, 0, 2)
        mask = _build_mask(edge_index, edge_type, edge_type_weights, x.dtype)
        scale = 1.0 / np.sqrt(D).astype(np.float32)
        scores = jnp.einsum('hnd,hmd->hnm', q2, k2) * scale + mask[None]
        attn = jax.nn.softmax(scores, axis=-1)
        out = jnp.einsum('hnm,hmd->hnd', attn, v2)
        out = out.transpose(1, 0, 2).reshape(N, OUT_F)
        return out @ wo.T + bo
    edge_index = jnp.stack([src, dst])
    h = jnp.maximum(_layernorm(x, axis=-1), 0.0)
    x = x + _L0_gnn_ref(h, edge_index, edge_type_5, L0_gnn_edge_type_weights, L0_gnn_wq, L0_gnn_bq, L0_gnn_wk, L0_gnn_bk, L0_gnn_wv, L0_gnn_bv, L0_gnn_wiq, L0_gnn_biq, L0_gnn_wik, L0_gnn_bik, L0_gnn_wiv, L0_gnn_biv, L0_gnn_wo, L0_gnn_bo)
    return x

_drawn_inputs = setup_inputs


def setup_inputs(seed=0):
    import zlib

    import numpy as np

    out = dict(_drawn_inputs(seed))
    spreads = {}
    factors = {'L0_gnn_edge_type_weights': 61.398,
     'L0_gnn_wq': 8.0,
     'L0_gnn_bq': 8.0,
     'L0_gnn_wk': 8.0,
     'L0_gnn_bk': 64.0,
     'L0_gnn_bv': 7.187,
     'L0_gnn_wiq': 8.0,
     'L0_gnn_biq': 35.58,
     'L0_gnn_wik': 8.0,
     'L0_gnn_bik': 64.0,
     'L0_gnn_biv': 4.526,
     'L0_gnn_bo': 2.887}
    for name, (base, spread) in spreads.items():
        noise = np.random.default_rng([zlib.crc32(name.encode()), seed]).standard_normal(out[name].shape)
        drawn = base * np.exp(spread * noise) if base else spread * noise
        out[name] = jnp.asarray(drawn.astype(out[name].dtype))
    for name, factor in factors.items():
        out[name] = (out[name] * factor).astype(out[name].dtype)
    return out
```

```python
from contextlib import ExitStack

import numpy as np
import concourse.bass as bass
from concourse import mybir

F32 = mybir.dt.float32
F32R = mybir.dt.float32r
F16 = mybir.dt.float16
BF16 = mybir.dt.bfloat16
I32 = mybir.dt.int32
ALU = mybir.AluOpType
ACT = mybir.ActivationFunctionType

P = 128
N = 384
F = 1024
H = 16
D = F // H
NT = N // P
KT = F // P
PAIRS = H // 2
E = 6528
ET = E // P
EG = 4
GROUPS = -(-ET // EG)
DST_ROW = 64
NW = 3 + 3 + 1
SLABS = NW * KT
HALF = 512
GS = F // HALF
KS = KT // GS
RAW = 3
RING = 4
AHEAD = RING - 1
HOTS = 2 * EG
EPS = 1e-5
LOW = -3.0e38
SCALE = 1.0 / float(np.sqrt(D))
EXP0 = 24
assert SCALE == 0.125 and H * D == F and ET * P == E and EXP0 + 4 * ET < 254

V0, VV0, Q0, K0, QK0, O0 = 0, KT, 2 * KT, 3 * KT, 4 * KT, 6 * KT
BQ, BK, BV, BIQ, BIK, BIV = (n * KT for n in range(6))
UNITS_FIRST = 2
UNITS_OF_SLAB = [2, 1, 1, 2, 1, 1, 2, 1]
assert UNITS_FIRST + sum(UNITS_OF_SLAB) == GROUPS


def tiles_of(group):
    return range(group * EG, min((group + 1) * EG, ET))


def gat_kernel(nc, slabs, x, edge_cols, edge_rows, edge_weights, biases, bo, out):
    with ExitStack() as ctx:
        def sb(name, shape, dt):
            return ctx.enter_context(nc.sbuf_tensor(name, shape, dt))

        def sem(name):
            return ctx.enter_context(nc.semaphore(name))

        x_sb = sb("x_sb", [P, NT, F], F32)
        a_hi = sb("a_hi", [P, KT, N], F32R)
        a_lo = sb("a_lo", [P, KT, N], F32R)
        b_hi = sb("b_hi", [P, KT, N], F32R)
        b_lo = sb("b_lo", [P, KT, N], F32R)
        c_hi = sb("c_hi", [P, KT, N], F32R)
        c_lo = sb("c_lo", [P, KT, N], F32R)
        v2 = sb("v2", [P, NT, PAIRS, 4, D], F32R)
        raw = sb("raw", [P, RAW, F], F32)
        w_hi = sb("w_hi", [P, RING, F], F32R)
        w_lo = sb("w_lo", [P, RING, F], F32R)
        qk_hi = sb("qk_hi", [P, 2, 2, N], F32R)
        qk_lo = sb("qk_lo", [P, 2, 2, N], F32R)
        work = sb("work", [P, NT * N + N], F32)
        prob = sb("prob", [P, 2, NT, N], F32)
        pt_hi = sb("pt_hi", [P, NT, N], F32R)
        pt_lo = sb("pt_lo", [P, NT, N], F32R)
        head_out = sb("head_out", [P, N], F32)
        bo_sb = sb("bo_sb", [P, F], F32)
        bias = sb("bias", [P, 6 * KT], F32)
        cols_i = sb("cols_i", [P, 3, ET], I32)
        cols = sb("cols", [P, 2, ET], F32)
        rows_i = sb("rows_i", [P, P], I32)
        rows = sb("rows", [P, P], F16)
        key = sb("key", [P, ET], F32)
        later = sb("later", [P, ET], F32)
        junk = sb("junk", [P, 2, P], BF16)
        expo = sb("expo", [P, ET], F32)
        live_expo = sb("live_expo", [P, ET], F32)
        value_bits = sb("value_bits", [P, ET], I32)
        type3 = sb("type3", [P, ET], I32)
        cls_e = sb("cls_e", [P, ET], I32)
        tile_expo = sb("tile_expo", [P, ET], F32)
        hot_dst = sb("hot_dst", [P, HOTS, N], BF16)
        iota = sb("iota", [P, N], F16)
        select = sb("select", [P, ET], F16)
        above = sb("above", [P, P], F16)
        ident = sb("ident", [P, P], F32)
        ew = sb("ew", [P, 4], F32)
        sp = sb("sp", [P, 5, 4], F32)
        stats = sb("stats", [P, NT, 2, 6], F32)
        mean_var = sb("mean_var", [P, NT, 2], F32)
        var_eps = sb("var_eps", [P, NT], F32)
        minus_half = sb("minus_half", [P, NT], F32)
        rstd = sb("rstd", [P, NT], F32)
        shift = sb("shift", [P, NT], F32)
        row_max = sb("row_max", [P, 2, NT], F32)
        neg_max = sb("neg_max", [P, 2, NT], F32)
        row_sum = sb("row_sum", [P, 2, NT], F32)
        row_inv = sb("row_inv", [P, 2, NT], F32)
        y = x_sb
        assert HOTS * N * 2 == (NT + 1) * N * 4
        hot_src = work[:, :].bitcast(BF16).rearrange("p (r n) -> p r n", n=N)
        mask = work[:, 0:NT * N].rearrange("p (t n) -> p t n", n=N)
        half_sum = work[:, NT * N:(NT + 1) * N]
        diag = prob[:, 0]
        pick = prob
        winner = x_sb[:, 0:2, :].rearrange("p a b -> p (a b)")[:, 0:NT * N].rearrange("p (t n) -> p t n", n=N)
        cls = x_sb[:, 1:3, :].rearrange("p a b -> p (a b)")[:, 2 * F - NT * N:].bitcast(I32).rearrange("p (t n) -> p t n", n=N)

        bank = [ctx.enter_context(nc.psum_tensor(f"bank{i}", [P, HALF], F32)) for i in range(8)]
        mask_bank = bank[0:3]
        key_bank = bank[6:8]
        h_bank = bank[3:6]
        tile_bank = bank[3:5]
        v2_bank = [bank[5:8], bank[0:3]]
        score_bank = bank[0:3]
        pt_bank = bank[5:8]
        pair_bank = bank[3]
        head_bank = bank[4]
        out_bank = [bank[0:3], bank[5:8]]

        edges_in, small_in, bo_in, y_in = sem("edges_in"), sem("small_in"), sem("bo_in"), sem("y_in")
        x_in = [sem(f"x_in{t}") for t in range(NT)]
        slab_in = [sem(f"slab_in{r}") for r in range(RAW)]
        const_step, iota_ok, select_ok, above_ok = sem("const_step"), sem("iota_ok"), sem("select_ok"), sem("above_ok")
        tile_expo_ok, ident_ok, diag_ok = sem("tile_expo_ok"), sem("ident_ok"), sem("diag_ok")
        edge_step, rows_ok, keys_done, later_ok, value_ok = (
            sem("edge_step"), sem("rows_ok"), sem("keys_done"), sem("later_ok"), sem("value_ok"))
        expo_live = sem("expo_live")
        hot_ok, hot_used = sem("hot_ok"), sem("hot_used")
        sp_step, sp_in, sp_exp, sp_ln, sp_ok = sem("sp_step"), sem("sp_in"), sem("sp_exp"), sem("sp_ln"), sem("sp_ok")
        mask_step, mask_ok = sem("mask_step"), sem("mask_ok")
        stats_step, stats_agg, var_ok, rstd_ok, shift_ok, h_ok = (
            sem("stats_step"), sem("stats_agg"), sem("var_ok"), sem("rstd_ok"), sem("shift_ok"), sem("h_ok"))
        h_turned, h_hi, h_lo = sem("h_turned"), sem("h_hi"), sem("h_lo")
        slab_hi, slab_lo, slab_used = sem("slab_hi"), sem("slab_lo"), sem("slab_used")
        tile_hi, tile_lo = sem("tile_hi"), sem("tile_lo")
        v2_done, v2_hi, v2_lo = sem("v2_done"), sem("v2_hi"), sem("v2_lo")
        score_done, masked, neg_max_ok = sem("score_done"), sem("masked"), sem("neg_max_ok")
        exp_done, inv_ok, prob_ok = sem("exp_done"), sem("inv_ok"), sem("prob_ok")
        pt_done, pt_hi_ok, pt_lo_ok = sem("pt_done"), sem("pt_hi_ok"), sem("pt_lo_ok")
        head_done, half_ok, head_sum, head_hi, head_lo = (
            sem("head_done"), sem("half_ok"), sem("head_sum"), sem("head_hi"), sem("head_lo"))
        y_ok, out_done, out_ok, stored = sem("y_ok"), sem("out_done"), sem("out_ok"), sem("stored")

        block = ctx.enter_context(nc.Block())

        def tile_place(t):
            stage, j = t // KT, t % KT
            if stage < 3:
                hi, lo, b = [(b_hi, b_lo, BV), (b_hi, b_lo, BQ), (c_hi, c_lo, BK)][stage]
                return hi[:, j, :], lo[:, j, :], b + j, tile_bank[t % 2]
            pair, which = (t - 3 * KT) // 2, t % 2
            return (qk_hi[:, pair % 2, which, :], qk_lo[:, pair % 2, which, :],
                    (BIQ, BIK)[which] + pair, pair_bank)

        def slab_of(t):
            return t if t < KT else t + KT

        def rows_of(h):
            own = (h % 2) * D
            return slice(own, own + D), slice(D - own, 2 * D - own)

        @block.sync
        def _(sp_eng):
            for t in range(NT):
                sp_eng.dma_start(x_sb[:, t, :], x[t * P:(t + 1) * P, :]).then_inc(x_in[t], 16)
            for s in range(SLABS):
                if s >= RAW:
                    sp_eng.wait_ge(slab_hi, s - RAW + 1)
                    sp_eng.wait_ge(slab_lo, s - RAW + 1)
                sp_eng.dma_start(raw[:, s % RAW, :], slabs[s]).then_inc(slab_in[s % RAW], 16)
                if s == VV0 + RAW:
                    sp_eng.wait_ge(h_turned, KT)
                    sp_eng.wait_ge(mask_ok, 1)
                    for t in range(NT):
                        sp_eng.dma_start(y[:, t, :], x[t * P:(t + 1) * P, :]).then_inc(y_in, 16)
            for g in range(GS):
                for t in range(NT):
                    sp_eng.wait_ge(out_ok, g * NT + t + 1)
                    sp_eng.dma_start(out[t * P:(t + 1) * P, g * HALF:(g + 1) * HALF],
                                     y[:, t, g * HALF:(g + 1) * HALF]).then_inc(stored, 16)
            sp_eng.wait_ge(stored, 16 * GS * NT)

        @block.gpsimd
        def _(pool):
            nc.gpsimd.iota(iota[:], pattern=[[1, N]], base=0, channel_multiplier=0,
                           allow_small_or_imprecise_dtypes=True).then_inc(iota_ok, 1)
            nc.gpsimd.memset(select[:], 0.0).then_inc(const_step, 1)
            nc.gpsimd.memset(above[:], 1.0).then_inc(const_step, 1)
            nc.gpsimd.memset(ident[:], 0.0).then_inc(const_step, 1)
            nc.gpsimd.memset(diag[:], 0.0).then_inc(const_step, 1)
            nc.gpsimd.memset(minus_half[:], -0.5).then_inc(const_step, 1)
            nc.gpsimd.iota(tile_expo[:], pattern=[[4, ET]], base=EXP0, channel_multiplier=0,
                           allow_small_or_imprecise_dtypes=True).then_inc(tile_expo_ok, 1)
            pool.wait_ge(const_step, 5)
            nc.gpsimd.affine_select(out=select[:], in_=select[:], compare_op=ALU.not_equal, fill=float(N),
                                    base=0, pattern=[[-1, ET]], channel_multiplier=1).then_inc(const_step, 1)
            pool.wait_ge(const_step, 6)
            nc.gpsimd.affine_select(out=select[:], in_=select[:], compare_op=ALU.not_equal, fill=1.0,
                                    base=-DST_ROW, pattern=[[-1, ET]], channel_multiplier=1).then_inc(select_ok, 1)
            nc.gpsimd.affine_select(out=above[:], in_=above[:], compare_op=ALU.is_gt, fill=0.0,
                                    base=0, pattern=[[1, P]], channel_multiplier=-1).then_inc(above_ok, 1)
            nc.gpsimd.affine_select(out=ident[:], in_=ident[:], compare_op=ALU.not_equal, fill=1.0,
                                    base=0, pattern=[[-1, P]], channel_multiplier=1).then_inc(ident_ok, 1)
            for t in range(NT):
                nc.gpsimd.affine_select(out=diag[:, t, :], in_=diag[:, t, :], compare_op=ALU.not_equal,
                                        fill=2.0 ** (EXP0 - 1 - 127), base=t * P, pattern=[[-1, N]],
                                        channel_multiplier=1).then_inc(diag_ok, 1)
            pool.wait_ge(var_ok, 1)
            nc.gpsimd.tensor_tensor(rstd[:], var_eps[:], minus_half[:], ALU.pow).then_inc(rstd_ok, 1)

            def split_lo(s):
                pool.wait_ge(slab_hi, s + 1)
                if s >= RING:
                    pool.wait_ge(slab_used, s - RING + 1)
                nc.gpsimd.tensor_tensor(w_lo[:, s % RING, :], raw[:, s % RAW, :],
                                        w_hi[:, s % RING, :].bitcast(F32), ALU.subtract).then_inc(slab_lo, 1)

            def pair_lo_part(pair):
                pool.wait_ge(head_hi, pair + 1)
                nc.gpsimd.tensor_tensor(a_lo[:, pair, :], head_out[:], a_hi[:, pair, :].bitcast(F32),
                                        ALU.subtract).then_inc(head_lo, 1)

            for s in range(QK0 + 2 + AHEAD):
                split_lo(s)
                if s == Q0 + AHEAD:
                    pool.wait_ge(y_in, 16 * NT)
                    pool.wait_ge(bo_in, 16)
                    for t in range(NT):
                        nc.gpsimd.tensor_tensor(y[:, t, :], y[:, t, :], bo_sb[:], ALU.add).then_inc(y_ok, 1)
            for i in range(H + 1):
                s = QK0 + 2 + AHEAD + i
                if s < O0 + RING:
                    split_lo(s)
                if i >= 3 and i % 2 == 1:
                    pair_lo_part((i - 3) // 2)
                if i < H:
                    pool.wait_ge(inv_ok, i + 1)
                    for t in range(NT):
                        nc.gpsimd.tensor_scalar(prob[:, i % 2, t, :], prob[:, i % 2, t, :],
                                                row_inv[:, i % 2, t:t + 1], 1.0, ALU.mult,
                                                ALU.mult).then_inc(prob_ok, 1)
            pair_lo_part(PAIRS - 1)
            for s in range(O0 + RING, SLABS):
                split_lo(s)

        @block.scalar
        def _(act):
            act.dma_start(cols_i[:], edge_cols).then_inc(edges_in, 16)
            act.dma_start(rows_i[:], edge_rows).then_inc(edges_in, 16)
            act.dma_start(ew[:], edge_weights.rearrange("(a n) -> a n", a=1).to_broadcast([P, 4])).then_inc(small_in, 16)
            act.dma_start(bias[:], biases).then_inc(small_in, 16)
            act.dma_start(bo_sb[:], bo.rearrange("(a n) -> a n", a=1).to_broadcast([P, F])).then_inc(bo_in, 16)
            act.wait_ge(sp_in, 1)
            nc.scalar.activation(sp[:, 2, :], sp[:, 1, :], ACT.Exp).then_inc(sp_exp, 1)
            act.wait_ge(sp_exp, 1)
            nc.scalar.activation(sp[:, 3, :], sp[:, 2, :], ACT.Ln, bias=1.0).then_inc(sp_ln, 1)
            act.wait_ge(shift_ok, 1)
            for t in range(NT):
                nc.scalar.activation(x_sb[:, t, :], x_sb[:, t, :], ACT.Relu, scale=rstd[:, t:t + 1],
                                     bias=shift[:, t:t + 1]).then_inc(h_ok, 1)

            def split_hi(s):
                act.wait_ge(slab_in[s % RAW], 16 * (s // RAW + 1))
                if s >= RING:
                    act.wait_ge(slab_used, s - RING + 1)
                nc.scalar.activation(w_hi[:, s % RING, :], raw[:, s % RAW, :], ACT.Copy).then_inc(slab_hi, 1)

            def tile_hi_part(t):
                hi, _, b, psum = tile_place(t)
                act.wait_ge(slab_used, slab_of(t) + 1)
                nc.scalar.activation(hi, psum[:, 0:N], ACT.Identity, bias=bias[:, b:b + 1]).then_inc(tile_hi, 1)

            split_hi(0)
            for k in range(KT):
                act.wait_ge(h_turned, k + 1)
                nc.scalar.activation(a_hi[:, k, :], h_bank[k % 3][:, 0:N], ACT.Copy).then_inc(h_hi, 1)
            for s in range(1, AHEAD):
                split_hi(s)
            act.wait_ge(small_in, 32)
            for s in range(QK0 + 2):
                split_hi(s + AHEAD)
                if s < VV0:
                    tile_hi_part(s)
                elif s < Q0:
                    g, k = (s - VV0) // KS, (s - VV0) % KS
                    if k == KS - 1:
                        for t in range(NT):
                            if t < NT - 1:
                                act.wait_ge(v2_done, g * (NT - 1) + t + 1)
                            else:
                                act.wait_ge(slab_used, s + 1)
                            pairs = PAIRS // GS
                            nc.scalar.activation(
                                v2[:, t, g * pairs:(g + 1) * pairs, 0:4:3, :],
                                v2_bank[g][t][:, :].rearrange("p (a b d) -> p a b d", b=2, d=D),
                                ACT.Copy).then_inc(v2_hi, 1)
                else:
                    tile_hi_part(s - KT)

            def pair_hi_part(pair):
                act.wait_ge(head_sum, 2 * pair + 2)
                nc.scalar.activation(a_hi[:, pair, :], head_out[:], ACT.Copy).then_inc(head_hi, 1)

            for i in range(H + 1):
                if i >= 3 and i % 2 == 1:
                    pair_hi_part((i - 3) // 2)
                if i >= 1:
                    for m in range(NT):
                        act.wait_ge(pt_done, (i - 1) * NT + m + 1)
                        nc.scalar.activation(pt_hi[:, m, :], pt_bank[m][:, 0:N], ACT.Copy).then_inc(pt_hi_ok, 1)
                if i < H:
                    act.wait_ge(neg_max_ok, i + 1)
                    for t in range(NT):
                        nc.scalar.activation(prob[:, i % 2, t, :], prob[:, i % 2, t, :], ACT.Exp, scale=SCALE,
                                             bias=neg_max[:, i % 2, t:t + 1],
                                             accum_out=row_sum[:, i % 2, t:t + 1]).then_inc(exp_done, 1)
                if QK0 + 2 + AHEAD + i < O0 + RING:
                    split_hi(QK0 + 2 + AHEAD + i)
                if i < 2 * PAIRS - 2:
                    tile_hi_part(3 * KT + 2 + i)
                if i >= 1:
                    own, other = rows_of(i - 1)
                    act.wait_ge(head_done, i)
                    b = BIV + (i - 1) // 2
                    nc.scalar.activation(half_sum[own, :], head_bank[other, 0:N], ACT.Identity,
                                         bias=bias[own, b:b + 1]).then_inc(half_ok, 1)
            pair_hi_part(PAIRS - 1)
            for s in range(O0 + RING, SLABS):
                split_hi(s)

        @block.vector
        def _(dve):
            dve.wait_ge(edges_in, 32)
            nc.vector.tensor_copy(rows[:], rows_i[:]).then_inc(rows_ok, 1)
            nc.vector.tensor_copy(cols[:], cols_i[:, 0:2, :]).then_inc(edge_step, 1)
            nc.vector.tensor_scalar(type3[:], cols_i[:, 2, :], 3, None, ALU.add).then_inc(edge_step, 1)
            dve.wait_ge(edge_step, 2)
            nc.vector.scalar_tensor_tensor(key[:], cols[:, 0, :], float(N), cols[:, 1, :],
                                           op0=ALU.mult, op1=ALU.add).then_inc(edge_step, 1)
            nc.vector.tensor_scalar(cls_e[:], type3[:], 3, None, ALU.bitwise_and).then_inc(edge_step, 1)
            dve.wait_ge(tile_expo_ok, 1)
            dve.wait_ge(edge_step, 4)
            nc.vector.tensor_tensor(expo[:], cls_e[:], tile_expo[:], ALU.add).then_inc(edge_step, 1)

            for t in range(NT):
                dve.wait_ge(x_in[t], 16)
                for b in range(2):
                    nc.vector.bn_stats(stats[:, t, b, :], x_sb[:, t, b * HALF:(b + 1) * HALF]).then_inc(stats_step, 1)
                dve.wait_ge(stats_step, 2 * (t + 1))
                nc.vector.bn_aggr(mean_var[:, t, :], stats[:, t, :, :]).then_inc(stats_agg, 1)
            dve.wait_ge(stats_agg, NT)
            nc.vector.tensor_scalar(var_eps[:], mean_var[:, :, 1], EPS, None, ALU.add).then_inc(var_ok, 1)

            dve.wait_ge(small_in, 32)
            nc.vector.tensor_scalar(sp[:, 0, :], ew[:], -1.0, None, ALU.mult).then_inc(sp_step, 1)
            dve.wait_ge(sp_step, 1)
            nc.vector.tensor_tensor(sp[:, 1, :], sp[:, 0, :], ew[:], ALU.min).then_inc(sp_in, 1)
            nc.vector.tensor_scalar(sp[:, 4, :], ew[:], 0.0, None, ALU.max).then_inc(sp_step, 1)

            dve.wait_ge(rstd_ok, 1)
            nc.vector.scalar_tensor_tensor(shift[:], mean_var[:, :, 0], -1.0, rstd[:],
                                           op0=ALU.mult, op1=ALU.mult).then_inc(shift_ok, 1)

            dve.wait_ge(sp_ln, 1)
            dve.wait_ge(sp_step, 2)
            nc.vector.tensor_tensor(sp[:, 0, :], sp[:, 3, :], sp[:, 4, :], ALU.add).then_inc(sp_step, 1)
            dve.wait_ge(sp_step, 3)
            nc.vector.tensor_scalar(sp[:, 1, :], sp[:, 0, :], 1.0 / SCALE, None, ALU.mult).then_inc(sp_ok, 1)

            def edge_unit(g):
                tiles = tiles_of(g)
                dve.wait_ge(keys_done, g + 1)
                dve.wait_ge(above_ok, 1)
                for t in tiles:
                    if t >= 2:
                        dve.wait_ge(later_ok, t - 1)
                    nc.vector.scalar_tensor_tensor(
                        junk[:, t % 2, :], key_bank[g % 2][:, (t % EG) * P:(t % EG + 1) * P], key[:, t:t + 1], above[:],
                        op0=ALU.is_equal, op1=ALU.mult, accum_out=later[:, t:t + 1]).then_inc(later_ok, 1)
                a, b = tiles[0], tiles[-1] + 1
                dve.wait_ge(later_ok, b)
                nc.vector.scalar_tensor_tensor(live_expo[:, a:b], later[:, a:b], 0.0, expo[:, a:b],
                                               op0=ALU.is_equal, op1=ALU.mult).then_inc(expo_live, 1)
                dve.wait_ge(expo_live, g + 1)
                nc.vector.tensor_scalar(value_bits[:, a:b], live_expo[:, a:b], float(1 << 23), None,
                                        ALU.mult).then_inc(value_ok, 1)
                dve.wait_ge(iota_ok, 1)
                for t in tiles:
                    if t >= HOTS:
                        dve.wait_ge(hot_used, t - HOTS + 1)
                    nc.vector.tensor_scalar(hot_src[:, t % HOTS, :], iota[:], cols[:, 0, t:t + 1], None,
                                            ALU.is_equal).then_inc(hot_ok, 1)
                    if t == a:
                        dve.wait_ge(value_ok, g + 1)
                    nc.vector.tensor_scalar(hot_dst[:, t % HOTS, :], iota[:], cols[:, 1, t:t + 1],
                                            value_bits[:, t:t + 1].bitcast(F32), ALU.is_equal,
                                            ALU.mult).then_inc(hot_ok, 1)

            def tile_lo_part(t):
                hi, lo, b, psum = tile_place(t)
                dve.wait_ge(tile_hi, t + 1)
                nc.vector.scalar_tensor_tensor(lo, psum[:, 0:N], bias[:, b:b + 1], hi.bitcast(F32),
                                               op0=ALU.add, op1=ALU.subtract).then_inc(tile_lo, 1)

            def build_mask():
                dve.wait_ge(hot_used, ET)
                dve.wait_ge(diag_ok, NT)
                for t in range(NT):
                    nc.vector.tensor_tensor(winner[:, t, :], mask_bank[t][:, 0:N], diag[:, t, :],
                                            ALU.max).then_inc(mask_step, 1)
                dve.wait_ge(mask_step, NT)
                nc.vector.tensor_scalar(cls[:], winner[:].bitcast(I32), 23, 3, ALU.logical_shift_right,
                                        ALU.bitwise_and).then_inc(mask_step, 1)
                nc.vector.tensor_scalar(mask[:], winner[:], 0.0, LOW, ALU.is_equal, ALU.mult).then_inc(mask_step, 1)
                dve.wait_ge(sp_ok, 1)
                for c in range(4):
                    dve.wait_ge(mask_step, NT + 2 + 2 * c)
                    nc.vector.tensor_scalar(pick[:, c % 2], cls[:], float(c), sp[:, 1, c:c + 1], ALU.is_equal,
                                            ALU.mult).then_inc(mask_step, 1)
                    dve.wait_ge(mask_step, NT + 3 + 2 * c)
                    nc.vector.tensor_tensor(mask[:], mask[:], pick[:, c % 2], ALU.add).then_inc(
                        mask_step if c < 3 else mask_ok, 1)

            for g in range(UNITS_FIRST):
                edge_unit(g)
            for k in range(KT):
                dve.wait_ge(h_hi, k + 1)
                nc.vector.tensor_tensor(a_lo[:, k, :], h_bank[k % 3][:, 0:N], a_hi[:, k, :].bitcast(F32),
                                        ALU.subtract).then_inc(h_lo, 1)
            unit = UNITS_FIRST
            for s in range(QK0 + 2):
                if s < VV0:
                    for _ in range(UNITS_OF_SLAB[s]):
                        edge_unit(unit)
                        unit += 1
                    tile_lo_part(s)
                    if s == VV0 - 1:
                        build_mask()
                elif s < Q0:
                    g, k = (s - VV0) // KS, (s - VV0) % KS
                    if k == KS - 1:
                        for t in range(NT):
                            dve.wait_ge(v2_hi, g * NT + t + 1)
                            pairs = slice(g * PAIRS // GS, (g + 1) * PAIRS // GS)
                            nc.vector.tensor_tensor(
                                v2[:, t, pairs, 1:3, :], v2_bank[g][t][:, :].rearrange("p (a b d) -> p a b d", b=2, d=D),
                                v2[:, t, pairs, 0:4:3, :].bitcast(F32), ALU.subtract).then_inc(v2_lo, 1)
                else:
                    tile_lo_part(s - KT)

            for i in range(H + 1):
                if i < H:
                    for t in range(NT):
                        dve.wait_ge(score_done, i * NT + t + 1)
                        if i == 0:
                            dve.wait_ge(mask_ok, 1)
                        nc.vector.tensor_tensor_reduce(
                            out=prob[:, i % 2, t, :], in0=score_bank[t][:, 0:N], in1=mask[:, t, :], scale=1.0,
                            scalar=-3.4e38, op0=ALU.add, op1=ALU.max,
                            accum_out=row_max[:, i % 2, t:t + 1]).then_inc(masked, 1)
                    dve.wait_ge(masked, (i + 1) * NT)
                    nc.vector.tensor_scalar(neg_max[:, i % 2, :], row_max[:, i % 2, :], -SCALE, None,
                                            ALU.mult).then_inc(neg_max_ok, 1)
                if i >= 1:
                    for m in range(NT):
                        dve.wait_ge(pt_hi_ok, (i - 1) * NT + m + 1)
                        nc.vector.tensor_tensor(pt_lo[:, m, :], pt_bank[m][:, 0:N], pt_hi[:, m, :].bitcast(F32),
                                                ALU.subtract).then_inc(pt_lo_ok, 1)
                if i < H:
                    dve.wait_ge(exp_done, (i + 1) * NT)
                    nc.vector.reciprocal(row_inv[:, i % 2, :], row_sum[:, i % 2, :]).then_inc(inv_ok, 1)
                if i < 2 * PAIRS - 2:
                    tile_lo_part(3 * KT + 2 + i)
                if i >= 1:
                    own, _ = rows_of(i - 1)
                    dve.wait_ge(half_ok, i)
                    if i >= 3:
                        dve.wait_ge(head_lo, (i - 1) // 2)
                    nc.vector.tensor_tensor(head_out[own, :], head_bank[own, 0:N], half_sum[own, :],
                                            ALU.add).then_inc(head_sum, 1)
            for g in range(GS):
                for t in range(NT):
                    if t < NT - 1:
                        dve.wait_ge(out_done, g * (NT - 1) + t + 1)
                    else:
                        dve.wait_ge(slab_used, O0 + (g + 1) * KS)
                    if g == t == 0:
                        dve.wait_ge(y_ok, NT)
                    part = slice(g * HALF, (g + 1) * HALF)
                    nc.vector.tensor_tensor(y[:, t, part], out_bank[g][t][:, :], y[:, t, part],
                                            ALU.add).then_inc(out_ok, 1)

        @block.tensor
        def _(pe):
            def products(psum, w, a, first, last):
                nc.tensor.matmul(psum, w[0], a[0], start=first, stop=False)
                nc.tensor.matmul(psum, w[0], a[1], start=False, stop=False)
                return nc.tensor.matmul(psum, w[1], a[0], start=False, stop=last)

            def keys(g):
                for t in tiles_of(g):
                    mm = nc.tensor.matmul(key_bank[g % 2][:, (t % EG) * P:(t % EG + 1) * P],
                                          select[:, t:t + 1].to_broadcast([P, P]), rows[:], start=True, stop=True)
                mm.then_inc(keys_done, 1)

            def edge_unit(g):
                for t in tiles_of(g):
                    pe.wait_ge(hot_ok, 2 * (t + 1))
                    for n in range(NT):
                        mm = nc.tensor.matmul(mask_bank[n][:, 0:N], hot_src[:, t % HOTS, n * P:(n + 1) * P],
                                              hot_dst[:, t % HOTS, :], start=(t == 0), stop=(t == ET - 1))
                    mm.then_inc(hot_used, 1)
                if g + 2 < GROUPS:
                    pe.wait_ge(later_ok, tiles_of(g)[-1] + 1)
                    keys(g + 2)

            def split_slab(s):
                pe.wait_ge(slab_hi, s + 1)
                pe.wait_ge(slab_lo, s + 1)
                return w_hi[:, s % RING, :], w_lo[:, s % RING, :]

            def tile(t, a_h, a_l):
                hi, lo = split_slab(slab_of(t))
                if t >= 3 * KT:
                    pe.wait_ge(tile_lo, t)
                elif t >= 2:
                    pe.wait_ge(tile_lo, t - 1)
                psum = tile_place(t)[3]
                for k in range(KT):
                    c = slice(k * P, (k + 1) * P)
                    mm = products(psum[:, 0:N], (hi[:, c], lo[:, c]), (a_h[:, k, :], a_l[:, k, :]), k == 0, k == KT - 1)
                mm.then_inc(slab_used, 1)

            def moving(s, base, a_h, a_l, banks, done):
                hi, lo = split_slab(s)
                g, part = (s - base) // KS, (s - base) % KS
                for n in range(NT):
                    m = slice(n * P, (n + 1) * P)
                    for b in range(GS):
                        k, c = part * GS + b, slice(b * HALF, (b + 1) * HALF)
                        mm = products(banks[g][n][:, :], (a_h[:, k, m], a_l[:, k, m]), (hi[:, c], lo[:, c]),
                                      k == 0, k == KT - 1)
                    if n == NT - 1:
                        mm.then_inc(slab_used, 1)
                    elif part == KS - 1:
                        mm.then_inc(done, 1)

            pe.wait_ge(rows_ok, 1)
            pe.wait_ge(select_ok, 1)
            keys(0)
            keys(1)
            for g in range(UNITS_FIRST):
                edge_unit(g)
            pe.wait_ge(h_ok, NT)
            pe.wait_ge(ident_ok, 1)
            for k in range(KT):
                if k >= 3:
                    pe.wait_ge(h_lo, k - 2)
                for t in range(NT):
                    mm = nc.tensor.transpose(h_bank[k % 3][:, t * P:(t + 1) * P], x_sb[:, t, k * P:(k + 1) * P], ident[:])
                mm.then_inc(h_turned, 1)
            pe.wait_ge(h_lo, KT)
            unit = UNITS_FIRST
            for t in range(KT):
                tile(t, a_hi, a_lo)
                for _ in range(UNITS_OF_SLAB[t]):
                    edge_unit(unit)
                    unit += 1
            for s in range(VV0, Q0):
                if s == VV0 + KS:
                    pe.wait_ge(mask_step, NT)
                if s - VV0 < KS:
                    pe.wait_ge(tile_lo, (s - VV0 + 1) * GS)
                moving(s, VV0, b_hi, b_lo, v2_bank, v2_done)
            for t in range(KT, 3 * KT):
                tile(t, a_hi, a_lo)

            def pair_tile(t):
                if t % 2 == 0:
                    tile(t, b_hi, b_lo)
                else:
                    tile(t, c_hi, c_lo)

            def scores(h):
                own, _ = rows_of(h)
                turn = h // 2 % 2
                if h % 2 == 0:
                    pe.wait_ge(tile_lo, 3 * KT + h + 2)
                for n in range(NT):
                    if h >= 1:
                        pe.wait_ge(masked, (h - 1) * NT + n + 1)
                    m = slice(n * P, (n + 1) * P)
                    products(score_bank[n][:, 0:N], (qk_hi[own, turn, 0, m], qk_lo[own, turn, 0, m]),
                             (qk_hi[own, turn, 1, :], qk_lo[own, turn, 1, :]), True, True).then_inc(score_done, 1)

            def turn_probs(h):
                pe.wait_ge(prob_ok, (h + 1) * NT)
                for m in range(NT):
                    if h >= 1:
                        pe.wait_ge(pt_lo_ok, (h - 1) * NT + m + 1)
                    for n in range(NT):
                        mm = nc.tensor.transpose(pt_bank[m][:, n * P:(n + 1) * P],
                                                 prob[:, h % 2, n, m * P:(m + 1) * P], ident[:])
                    mm.then_inc(pt_done, 1)

            def heads_values(h):
                pair = h // 2
                if h >= 1:
                    pe.wait_ge(head_sum, h)
                for m in range(NT):
                    pe.wait_ge(pt_lo_ok, h * NT + m + 1)
                    w = v2[:, m, pair, 2 * (h % 2):2 * (h % 2) + 2, :]
                    nc.tensor.matmul(head_bank[:, 0:N], w, pt_hi[:, m, :], start=(m == 0), stop=False)
                    mm = nc.tensor.matmul(head_bank[:, 0:N], w, pt_lo[:, m, :], start=False, stop=(m == NT - 1))
                mm.then_inc(head_done, 1)

            pe.wait_ge(v2_lo, GS * NT)
            pair_tile(3 * KT)
            pair_tile(3 * KT + 1)
            for i in range(H + 1):
                if i < H:
                    scores(i)
                if i >= 1:
                    turn_probs(i - 1)
                if i < H - 2:
                    pair_tile(3 * KT + 2 + i)
                if i >= 1:
                    heads_values(i - 1)
            for s in range(O0, SLABS):
                if s < O0 + KS:
                    pe.wait_ge(head_lo, GS * (s - O0 + 1))
                moving(s, O0, a_hi, a_lo, out_bank, out_done)


def kernel(x, src, dst, edge_type_5, L0_gnn_edge_type_weights, L0_gnn_wq, L0_gnn_bq, L0_gnn_wk, L0_gnn_bk,
           L0_gnn_wv, L0_gnn_bv, L0_gnn_wiq, L0_gnn_biq, L0_gnn_wik, L0_gnn_bik, L0_gnn_wiv, L0_gnn_biv,
           L0_gnn_wo, L0_gnn_bo):
    import concourse.bacc as bacc
    from concourse.bass_utils import run_bass_kernel_spmd

    def stay(w):
        return np.asarray(w).reshape(KT, P, KT, P).transpose(0, 3, 2, 1).reshape(KT, P, F)

    def move(w):
        return np.asarray(w).reshape(GS, HALF, KS, GS, P).transpose(0, 2, 4, 3, 1).reshape(KT, P, F)

    second = np.stack([stay(L0_gnn_wiq), stay(L0_gnn_wik)], axis=1).reshape(2 * KT, P, F)
    slabs = np.concatenate([stay(L0_gnn_wv), move(L0_gnn_wiv), stay(L0_gnn_wq), stay(L0_gnn_wk), second,
                            move(L0_gnn_wo)])
    edges = [np.asarray(a).reshape(ET, P) for a in (src, dst, edge_type_5)]
    rows = np.zeros((P, P), edges[0].dtype)
    rows[0:ET], rows[DST_ROW:DST_ROW + ET] = edges[0], edges[1]
    biases = np.concatenate([np.asarray(b).reshape(KT, P) for b in (
        L0_gnn_bq, L0_gnn_bk, L0_gnn_bv, L0_gnn_biq, L0_gnn_bik, L0_gnn_biv)]).T
    arrays = {
        "in_slabs": slabs, "in_x": np.asarray(x), "in_edge_cols": np.stack(edges).transpose(2, 0, 1),
        "in_edge_rows": rows, "in_edge_weights": np.asarray(L0_gnn_edge_type_weights), "in_biases": biases,
        "in_bo": np.asarray(L0_gnn_bo),
    }
    arrays = {name: np.ascontiguousarray(a) for name, a in arrays.items()}
    nc = bacc.Bacc("TRN2", target_bir_lowering=False, num_devices=1)
    args = [nc.dram_tensor(name, a.shape, mybir.dt.from_np(a.dtype), kind="ExternalInput").ap()
            for name, a in arrays.items()]
    out = nc.dram_tensor("out_y", (N, F), F32, kind="ExternalOutput").ap()
    gat_kernel(nc, *args, out)
    return run_bass_kernel_spmd(nc, [arrays], core_ids=[0]).results[0]["out_y"]
```

```python
from contextlib import ExitStack

import numpy as np
import concourse.bass as bass
from concourse import mybir

F32 = mybir.dt.float32
F32R = mybir.dt.float32r
F16 = mybir.dt.float16
BF16 = mybir.dt.bfloat16
I32 = mybir.dt.int32
ALU = mybir.AluOpType
ACT = mybir.ActivationFunctionType

P = 128
N = 384
F = 1024
H = 16
D = F // H
NT = N // P
KT = F // P
PAIRS = H // 2
E = 6528
ET = E // P
EG = 4
GROUPS = -(-ET // EG)
DST_ROW = 64
NW = 3 + 3 + 1
SLABS = NW * KT
HALF = 512
GS = F // HALF
KS = KT // GS
RAW = 3
RING = 4
AHEAD = RING - 1
HOTS = 2 * EG
EPS = 1e-5
LOW = -3.0e38
SCALE = 1.0 / float(np.sqrt(D))
EXP0 = 24
assert SCALE == 0.125 and H * D == F and ET * P == E and EXP0 + 4 * ET < 254

V0, VV0, Q0, K0, QK0, O0 = 0, KT, 2 * KT, 3 * KT, 4 * KT, 6 * KT
BQ, BK, BV, BIQ, BIK, BIV = (n * KT for n in range(6))
HOT_FROM = 2
UNITS_OF_SLAB = [0, 2, 1, 2, 2, 1, 2, 2]
PAIRS_BY_POOL = PAIRS - 2
TILES_AHEAD = 3
assert 1 + sum(UNITS_OF_SLAB) == GROUPS


def tiles_of(group):
    return range(group * EG, min((group + 1) * EG, ET))


def gat_kernel(nc, slabs, x, edge_cols, edge_rows, edge_weights, biases, bo, out):
    with ExitStack() as ctx:
        def sb(name, shape, dt):
            return ctx.enter_context(nc.sbuf_tensor(name, shape, dt))

        def sem(name):
            return ctx.enter_context(nc.semaphore(name))

        x_sb = sb("x_sb", [P, NT, F], F32)
        a_hi = sb("a_hi", [P, KT, N], F32R)
        a_lo = sb("a_lo", [P, KT, N], F32R)
        b_hi = sb("b_hi", [P, KT, N], F32R)
        b_lo = sb("b_lo", [P, KT, N], F32R)
        c_hi = sb("c_hi", [P, KT, N], F32R)
        c_lo = sb("c_lo", [P, KT, N], F32R)
        v2 = sb("v2", [P, NT, PAIRS, 4, D], F32R)
        raw = sb("raw", [P, RAW, F], F32)
        w_hi = sb("w_hi", [P, RING, F], F32R)
        w_lo = sb("w_lo", [P, RING, F], F32R)
        q2 = sb("q2", [P, 2, 2, N], F32R)
        k2_hi = sb("k2_hi", [P, 2, 2, N], F32R)
        k2_lo = sb("k2_lo", [P, 2, 2, N], F32R)
        work = sb("work", [P, NT * N + N], F32)
        prob = sb("prob", [P, 2, NT, N], F32)
        pt_hi = sb("pt_hi", [P, NT, N], F32R)
        pt_lo = sb("pt_lo", [P, NT, N], F32R)
        work2 = sb("work2", [P, NT * N + N], F32)
        bias = sb("bias", [P, 6 * KT], F32)
        cols_i = sb("cols_i", [P, 3, ET], I32)
        cols = sb("cols", [P, 2, ET], F32)
        rows_i = sb("rows_i", [P, P], I32)
        rows = sb("rows", [P, P], F16)
        key = sb("key", [P, ET], F32)
        later = sb("later", [P, ET], F32)
        junk = sb("junk", [P, 2, P], BF16)
        expo = sb("expo", [P, ET], F32)
        live_expo = sb("live_expo", [P, ET], F32)
        value_bits = sb("value_bits", [P, ET], I32)
        type3 = sb("type3", [P, ET], I32)
        cls_e = sb("cls_e", [P, ET], I32)
        tile_expo = sb("tile_expo", [P, ET], F32)
        iota = sb("iota", [P, N], F16)
        select = sb("select", [P, ET], F16)
        above = sb("above", [P, P], F16)
        ident = sb("ident", [P, P], F32)
        ew = sb("ew", [P, 4], F32)
        sp = sb("sp", [P, 5, 4], F32)
        stats = sb("stats", [P, NT, 2, 6], F32)
        mean_var = sb("mean_var", [P, NT, 2], F32)
        var_eps = sb("var_eps", [P, NT], F32)
        minus_half = sb("minus_half", [P, NT], F32)
        rstd = sb("rstd", [P, NT], F32)
        shift = sb("shift", [P, NT], F32)
        row_max = sb("row_max", [P, 2, NT], F32)
        neg_max = sb("neg_max", [P, 2, NT], F32)
        row_sum = sb("row_sum", [P, 2, NT], F32)
        row_inv = sb("row_inv", [P, 2, NT], F32)
        y = x_sb
        assert HOTS * N * 2 == (NT + 1) * N * 4
        hot_src = work[:, :].bitcast(BF16).rearrange("p (r n) -> p r n", n=N)
        mask = work[:, 0:NT * N].rearrange("p (t n) -> p t n", n=N)
        half_sum = work[:, NT * N:(NT + 1) * N]
        hot_dst = work2[:, :].bitcast(BF16).rearrange("p (r n) -> p r n", n=N)
        bo_sb = work2[:, 0:F]
        head_out = work2[:, F:F + N]
        diag = prob[:, 0]
        pick = prob
        winner = x_sb[:, 0:2, :].rearrange("p a b -> p (a b)")[:, 0:NT * N].rearrange("p (t n) -> p t n", n=N)
        cls = x_sb[:, 1:3, :].rearrange("p a b -> p (a b)")[:, 2 * F - NT * N:].bitcast(I32).rearrange("p (t n) -> p t n", n=N)

        bank = [ctx.enter_context(nc.psum_tensor(f"bank{i}", [P, HALF], F32)) for i in range(8)]
        mask_bank = bank[0:3]
        key_bank = bank[6:8]
        h_bank = [bank[5], bank[4], bank[7]]
        tile_bank = bank[3:5]
        v2_bank = [bank[5:8], bank[0:3]]
        score_bank = bank[0:3]
        pt_bank = bank[5:8]
        pair_bank = bank[3]
        head_bank = bank[4]
        out_bank = [[bank[3], bank[0], bank[1]], [bank[2], bank[5], bank[6]]]

        edges_in, small_in, y_in = sem("edges_in"), sem("small_in"), sem("y_in")
        x_half_in = sem("x_half_in")
        x_in = [sem(f"x_in{t}") for t in range(NT)]
        slab_in = [sem(f"slab_in{r}") for r in range(RAW)]
        const_step, iota_ok, select_ok, above_ok = sem("const_step"), sem("iota_ok"), sem("select_ok"), sem("above_ok")
        tile_expo_ok, ident_ok, diag_ok = sem("tile_expo_ok"), sem("ident_ok"), sem("diag_ok")
        edge_step, rows_ok, keys_done, later_ok, value_ok = (
            sem("edge_step"), sem("rows_ok"), sem("keys_done"), sem("later_ok"), sem("value_ok"))
        expo_live = sem("expo_live")
        hot_ok, hot_used = sem("hot_ok"), sem("hot_used")
        sp_step, sp_in, sp_exp, sp_ln, sp_ok = sem("sp_step"), sem("sp_in"), sem("sp_exp"), sem("sp_ln"), sem("sp_ok")
        mask_step, mask_ok = sem("mask_step"), sem("mask_ok")
        stats_step, stats_agg, var_ok, rstd_ok, shift_ok, h_ok = (
            sem("stats_step"), sem("stats_agg"), sem("var_ok"), sem("rstd_ok"), sem("shift_ok"), sem("h_ok"))
        h_turned, h_hi, h_lo = sem("h_turned"), sem("h_hi"), sem("h_lo")
        half_hi, half_lo = sem("half_hi"), sem("half_lo")
        slab_hi, slab_lo, slab_used = sem("slab_hi"), sem("slab_lo"), sem("slab_used")
        tile_hi, tile_lo, k2_step = sem("tile_hi"), sem("tile_lo"), sem("k2_step")
        k2_read = sem("k2_read")
        v2_done, v2_hi, v2_lo = sem("v2_done"), sem("v2_hi"), sem("v2_lo")
        score_done, masked, neg_max_ok = sem("score_done"), sem("masked"), sem("neg_max_ok")
        exp_done, inv_ok, prob_ok = sem("exp_done"), sem("inv_ok"), sem("prob_ok")
        pt_done, pt_hi_ok, pt_lo_ok = sem("pt_done"), sem("pt_hi_ok"), sem("pt_lo_ok")
        head_done, half_ok, head_sum, head_hi, head_lo = (
            sem("head_done"), sem("half_ok"), sem("head_sum"), sem("head_hi"), sem("head_lo"))
        y_ok, out_done, out_ok, stored = sem("y_ok"), sem("out_done"), sem("out_ok"), sem("stored")

        block = ctx.enter_context(nc.Block())

        def tile_place(t):
            stage, j = t // KT, t % KT
            if stage < 3:
                hi, lo, b = [(b_hi, b_lo, BV), (b_hi, b_lo, BQ), (c_hi, c_lo, BK)][stage]
                return hi[:, j, :], lo[:, j, :], b + j, tile_bank[t % 2]
            pair, which = (t - 3 * KT) // 2, t % 2
            return None, None, (BIQ, BIK)[which] + pair, bank[4] if t - 3 * KT in (1, 3) else pair_bank

        def tile_hi_count(t):
            return t + 1 + max(0, t + 1 - 3 * KT)

        def split_place(s):
            j = s - O0 - KS
            if j < 0:
                return w_hi[:, s % RING, :], w_lo[:, s % RING, :]
            hi, lo = (b_hi, b_lo) if j < 3 else (c_hi, c_lo)
            part = slice(j % 3 * F, (j % 3 + 1) * F)
            return tuple(a[:, :, :].rearrange("p k n -> p (k n)")[:, part] for a in (hi, lo))

        def wait_split_place(eng, s):
            if s >= O0 + KS:
                eng.wait_ge(slab_used, O0)
            elif s >= RING:
                eng.wait_ge(slab_used, s - RING + 1)

        def slabs_of_step(i):
            first = QK0 + TILES_AHEAD + AHEAD + i
            return range(first + (i == H), min(first + 1 + (i >= H - 1), SLABS))

        def slab_of(t):
            return t if t < KT else t + KT

        def rows_of(h):
            own = (h % 2) * D
            return slice(own, own + D), slice(D - own, 2 * D - own)

        @block.sync
        def _(sp_eng):
            sp_eng.dma_start(rows_i[:], edge_rows).then_inc(edges_in, 16)
            sp_eng.dma_start(cols_i[:], edge_cols).then_inc(edges_in, 16)
            sp_eng.dma_start(x_sb[:, 0, 0:HALF], x[0:P, 0:HALF]).then_inc(x_half_in, 16)
            sp_eng.dma_start(x_sb[:, 0, HALF:F], x[0:P, HALF:F]).then_inc(x_in[0], 16)
            for t in range(1, NT):
                sp_eng.dma_start(x_sb[:, t, :], x[t * P:(t + 1) * P, :]).then_inc(x_in[t], 16)
            for s in range(SLABS):
                if s >= RAW:
                    sp_eng.wait_ge(slab_lo, s - RAW + 1)
                sp_eng.dma_start(raw[:, s % RAW, :], slabs[s]).then_inc(slab_in[s % RAW], 16)
                if s == 0:
                    sp_eng.dma_start(bias[:], biases).then_inc(small_in, 16)
                    sp_eng.dma_start(ew[:], edge_weights.rearrange("(a n) -> a n", a=1).to_broadcast([P, 4])).then_inc(small_in, 16)
                if s == Q0 + 2:
                    sp_eng.wait_ge(h_turned, KT)
                    sp_eng.wait_ge(mask_ok, 1)
                    for t in range(NT):
                        sp_eng.dma_start(y[:, t, :], x[t * P:(t + 1) * P, :]).then_inc(y_in, 16)
                    sp_eng.dma_start(bo_sb, bo.rearrange("(a n) -> a n", a=1).to_broadcast([P, F])).then_inc(y_in, 16)
            for g in range(GS):
                for t in range(NT):
                    sp_eng.wait_ge(out_ok, g * NT + t + 1)
                    sp_eng.dma_start(out[t * P:(t + 1) * P, g * HALF:(g + 1) * HALF],
                                     y[:, t, g * HALF:(g + 1) * HALF]).then_inc(stored, 16)
            sp_eng.wait_ge(stored, 16 * GS * NT)

        @block.gpsimd
        def _(pool):
            nc.gpsimd.iota(iota[:], pattern=[[1, N]], base=0, channel_multiplier=0,
                           allow_small_or_imprecise_dtypes=True).then_inc(iota_ok, 1)
            nc.gpsimd.memset(select[:], 0.0).then_inc(const_step, 1)
            nc.gpsimd.memset(above[:], 1.0).then_inc(const_step, 1)
            nc.gpsimd.memset(ident[:], 0.0).then_inc(const_step, 1)
            nc.gpsimd.memset(diag[:], 0.0).then_inc(const_step, 1)
            nc.gpsimd.memset(minus_half[:], -0.5).then_inc(const_step, 1)
            nc.gpsimd.iota(tile_expo[:], pattern=[[4, ET]], base=EXP0, channel_multiplier=0,
                           allow_small_or_imprecise_dtypes=True).then_inc(tile_expo_ok, 1)
            pool.wait_ge(const_step, 5)
            nc.gpsimd.affine_select(out=select[:], in_=select[:], compare_op=ALU.not_equal, fill=float(N),
                                    base=0, pattern=[[-1, ET]], channel_multiplier=1).then_inc(const_step, 1)
            pool.wait_ge(const_step, 6)
            nc.gpsimd.affine_select(out=select[:], in_=select[:], compare_op=ALU.not_equal, fill=1.0,
                                    base=-DST_ROW, pattern=[[-1, ET]], channel_multiplier=1).then_inc(select_ok, 1)
            nc.gpsimd.affine_select(out=above[:], in_=above[:], compare_op=ALU.is_gt, fill=0.0,
                                    base=0, pattern=[[1, P]], channel_multiplier=-1).then_inc(above_ok, 1)
            nc.gpsimd.affine_select(out=ident[:], in_=ident[:], compare_op=ALU.not_equal, fill=1.0,
                                    base=0, pattern=[[-1, P]], channel_multiplier=1).then_inc(ident_ok, 1)
            for t in range(NT):
                nc.gpsimd.affine_select(out=diag[:, t, :], in_=diag[:, t, :], compare_op=ALU.not_equal,
                                        fill=2.0 ** (EXP0 - 1 - 127), base=t * P, pattern=[[-1, N]],
                                        channel_multiplier=1).then_inc(diag_ok, 1)
            for t in range(NT):
                pool.wait_ge(var_ok, t + 1)
                nc.gpsimd.tensor_tensor(rstd[:, t:t + 1], var_eps[:, t:t + 1], minus_half[:, 0:1],
                                        ALU.pow).then_inc(rstd_ok, 1)

            def split_lo(s):
                pool.wait_ge(slab_hi, s + 1)
                hi, lo = split_place(s)
                nc.gpsimd.tensor_tensor(lo, raw[:, s % RAW, :], hi.bitcast(F32), ALU.subtract).then_inc(slab_lo, 1)

            def pair_lo_part(pair):
                pool.wait_ge(head_hi, pair + 1)
                nc.gpsimd.tensor_tensor(a_lo[:, pair, :], head_out, a_hi[:, pair, :].bitcast(F32),
                                        ALU.subtract).then_inc(head_lo, 1)

            for b in range(2):
                half = slice(b * HALF, (b + 1) * HALF)
                pool.wait_ge((half_hi, slab_hi)[b], 1)
                nc.gpsimd.tensor_tensor(w_lo[:, 0, half], raw[:, 0, half], w_hi[:, 0, half].bitcast(F32),
                                        ALU.subtract).then_inc((half_lo, slab_lo)[b], 1)
            for s in range(1, QK0 + TILES_AHEAD + AHEAD):
                split_lo(s)
                if s == Q0 + 2 * AHEAD:
                    pool.wait_ge(y_in, 16 * (NT + 1))
                    for t in range(NT):
                        nc.gpsimd.tensor_tensor(y[:, t, :], y[:, t, :], bo_sb, ALU.add).then_inc(y_ok, 1)
            for i in range(H + 1):
                if i >= 3 and i % 2 == 1 and (i - 3) // 2 < PAIRS_BY_POOL:
                    pair_lo_part((i - 3) // 2)
                if i < H:
                    for t in range(NT if i < H - TILES_AHEAD else 1):
                        pool.wait_ge(inv_ok, i * NT + t + 1)
                        nc.gpsimd.tensor_scalar(prob[:, i % 2, t, :], prob[:, i % 2, t, :],
                                                row_inv[:, i % 2, t:t + 1], 1.0, ALU.mult,
                                                ALU.mult).then_inc(prob_ok, 1)
                for s in slabs_of_step(i):
                    split_lo(s)

        @block.scalar
        def _(act):
            def split_hi(s):
                act.wait_ge(slab_in[s % RAW], 16 * (s // RAW + 1))
                wait_split_place(act, s)
                nc.scalar.activation(split_place(s)[0], raw[:, s % RAW, :], ACT.Copy).then_inc(slab_hi, 1)

            def tile_hi_part(t):
                hi, _, b, psum = tile_place(t)
                act.wait_ge(slab_used, slab_of(t) + 1)
                if t < 3 * KT:
                    nc.scalar.activation(hi, psum[:, 0:N], ACT.Identity, bias=bias[:, b:b + 1]).then_inc(tile_hi, 1)
                    return
                turn, dst = (t - 3 * KT) // 2 % 2, (q2, k2_hi)[t % 2]
                for h in range(2):
                    own, _ = rows_of(h)
                    nc.scalar.activation(dst[own, turn, h, :], psum[own, 0:N], ACT.Identity,
                                         bias=bias[own, b:b + 1]).then_inc(tile_hi, 1)

            def first_slab_hi(b):
                half = slice(b * HALF, (b + 1) * HALF)
                act.wait_ge(slab_in[0], 16)
                nc.scalar.activation(w_hi[:, 0, half], raw[:, 0, half], ACT.Copy).then_inc((half_hi, slab_hi)[b], 1)

            for t in range(NT):
                if t == NT - 1:
                    first_slab_hi(0)
                act.wait_ge(shift_ok, t + 1)
                for part in (slice(0, F),) if t < NT - 1 else (slice(0, HALF), slice(HALF, F)):
                    nc.scalar.activation(x_sb[:, t, part], x_sb[:, t, part], ACT.Relu, scale=rstd[:, t:t + 1],
                                         bias=shift[:, t:t + 1]).then_inc(h_ok, 1)
            for k in range(KT):
                act.wait_ge(h_turned, k + 1)
                nc.scalar.activation(a_hi[:, k, :], h_bank[k % 3][:, 0:N], ACT.Copy).then_inc(h_hi, 1)
                if k == 0:
                    first_slab_hi(1)
            for s in range(1, AHEAD):
                split_hi(s)
            act.wait_ge(small_in, 32)
            for s in range(QK0 + TILES_AHEAD):
                split_hi(s + AHEAD)
                if s < VV0:
                    tile_hi_part(s)
                    if s == 2:
                        act.wait_ge(sp_in, 1)
                        nc.scalar.activation(sp[:, 2, :], sp[:, 1, :], ACT.Exp).then_inc(sp_exp, 1)
                        act.wait_ge(sp_exp, 1)
                        nc.scalar.activation(sp[:, 3, :], sp[:, 2, :], ACT.Ln, bias=1.0).then_inc(sp_ln, 1)
                        act.wait_ge(sp_ln, 1)
                        nc.scalar.activation(sp[:, 2, :], sp[:, 1, :], ACT.Exp).then_inc(sp_exp, 1)
                elif s < Q0:
                    g, k = (s - VV0) // KS, (s - VV0) % KS
                    if k == KS - 1:
                        for t in range(NT):
                            if t < NT - 1:
                                act.wait_ge(v2_done, g * (NT - 1) + t + 1)
                            else:
                                act.wait_ge(slab_used, s + 1)
                            pairs = PAIRS // GS
                            nc.scalar.activation(
                                v2[:, t, g * pairs:(g + 1) * pairs, 0:4:3, :],
                                v2_bank[g][t][:, :].rearrange("p (a b d) -> p a b d", b=2, d=D),
                                ACT.Copy).then_inc(v2_hi, 1)
                else:
                    tile_hi_part(s - KT)

            def pair_hi_part(pair):
                act.wait_ge(head_sum, 2 * pair + 2)
                nc.scalar.activation(a_hi[:, pair, :], head_out, ACT.Copy).then_inc(head_hi, 1)

            for i in range(H + 1):
                if i >= 3 and i % 2 == 1:
                    pair_hi_part((i - 3) // 2)
                if i >= 1:
                    for m in range(NT):
                        act.wait_ge(pt_done, (i - 1) * NT + m + 1)
                        nc.scalar.activation(pt_hi[:, m, :], pt_bank[m][:, 0:N], ACT.Copy).then_inc(pt_hi_ok, 1)
                if i < H:
                    for t in range(NT):
                        act.wait_ge(neg_max_ok, i * NT + t + 1)
                        nc.scalar.activation(prob[:, i % 2, t, :], prob[:, i % 2, t, :], ACT.Exp, scale=SCALE,
                                             bias=neg_max[:, i % 2, t:t + 1],
                                             accum_out=row_sum[:, i % 2, t:t + 1]).then_inc(exp_done, 1)
                for s in slabs_of_step(i):
                    split_hi(s)
                if i < H - TILES_AHEAD:
                    tile_hi_part(3 * KT + TILES_AHEAD + i)
                if i >= 1:
                    own, other = rows_of(i - 1)
                    act.wait_ge(head_done, i)
                    b = BIV + (i - 1) // 2
                    nc.scalar.activation(half_sum[own, :], head_bank[other, 0:N], ACT.Identity,
                                         bias=bias[own, b:b + 1]).then_inc(half_ok, 1)
            pair_hi_part(PAIRS - 1)

        @block.vector
        def _(dve):
            dve.wait_ge(edges_in, 32)
            nc.vector.tensor_copy(rows[:], rows_i[:]).then_inc(rows_ok, 1)
            nc.vector.tensor_copy(cols[:], cols_i[:, 0:2, :]).then_inc(edge_step, 1)
            nc.vector.tensor_scalar(type3[:], cols_i[:, 2, :], 3, None, ALU.add).then_inc(edge_step, 1)
            dve.wait_ge(edge_step, 2)
            nc.vector.scalar_tensor_tensor(key[:], cols[:, 0, :], float(N), cols[:, 1, :],
                                           op0=ALU.mult, op1=ALU.add).then_inc(edge_step, 1)
            nc.vector.tensor_scalar(cls_e[:], type3[:], 3, None, ALU.bitwise_and).then_inc(edge_step, 1)
            dve.wait_ge(tile_expo_ok, 1)
            dve.wait_ge(edge_step, 4)
            nc.vector.tensor_tensor(expo[:], cls_e[:], tile_expo[:], ALU.add).then_inc(edge_step, 1)

            def shift_part(t):
                dve.wait_ge(rstd_ok, t + 1)
                nc.vector.scalar_tensor_tensor(shift[:, t:t + 1], mean_var[:, t, 0:1], -1.0, rstd[:, t:t + 1],
                                               op0=ALU.mult, op1=ALU.mult).then_inc(shift_ok, 1)

            def edge_unit_later(g, tiles):
                dve.wait_ge(keys_done, g + 1)
                dve.wait_ge(above_ok, 1)
                for t in tiles:
                    if t >= 2:
                        dve.wait_ge(later_ok, t - 1)
                    nc.vector.scalar_tensor_tensor(
                        junk[:, t % 2, :], key_bank[g % 2][:, (t % EG) * P:(t % EG + 1) * P], key[:, t:t + 1], above[:],
                        op0=ALU.is_equal, op1=ALU.mult, accum_out=later[:, t:t + 1]).then_inc(later_ok, 1)

            def edge_unit_values(g):
                tiles = tiles_of(g)
                a, b = tiles[0], tiles[-1] + 1
                dve.wait_ge(later_ok, b)
                nc.vector.scalar_tensor_tensor(live_expo[:, a:b], later[:, a:b], 0.0, expo[:, a:b],
                                               op0=ALU.is_equal, op1=ALU.mult).then_inc(expo_live, 1)
                dve.wait_ge(expo_live, g + 1)
                nc.vector.tensor_scalar(value_bits[:, a:b], live_expo[:, a:b], float(1 << 23), None,
                                        ALU.mult).then_inc(value_ok, 1)

            def edge_tile_hot(t):
                dve.wait_ge(iota_ok, 1)
                if t >= HOTS:
                    dve.wait_ge(hot_used, t - HOTS + 1)
                nc.vector.tensor_scalar(hot_src[:, t % HOTS, :], iota[:], cols[:, 0, t:t + 1], None,
                                        ALU.is_equal).then_inc(hot_ok, 1)
                if t % EG == 0:
                    dve.wait_ge(value_ok, t // EG + 1)
                nc.vector.tensor_scalar(hot_dst[:, t % HOTS, :], iota[:], cols[:, 1, t:t + 1],
                                        value_bits[:, t:t + 1].bitcast(F32), ALU.is_equal,
                                        ALU.mult).then_inc(hot_ok, 1)

            def edge_unit(g):
                edge_unit_later(g, tiles_of(g))
                edge_unit_values(g)
                for t in tiles_of(g):
                    edge_tile_hot(t)

            for t in range(NT):
                for b in range(2):
                    if t == 0:
                        dve.wait_ge((x_half_in, x_in[0])[b], 16)
                    elif b == 0:
                        dve.wait_ge(x_in[t], 16)
                    nc.vector.bn_stats(stats[:, t, b, :], x_sb[:, t, b * HALF:(b + 1) * HALF]).then_inc(stats_step, 1)
                    if t >= 1 and b == 0:
                        shift_part(t - 1)
                dve.wait_ge(stats_step, 2 * (t + 1))
                nc.vector.bn_aggr(mean_var[:, t, :], stats[:, t, :, :]).then_inc(stats_agg, 1)
                dve.wait_ge(stats_agg, t + 1)
                nc.vector.tensor_scalar(var_eps[:, t:t + 1], mean_var[:, t, 1:2], EPS, None, ALU.add).then_inc(var_ok, 1)
                edge_unit_later(0, range(t, t + 1))
            shift_part(NT - 1)
            edge_unit_later(0, range(NT, EG))

            def softplus_in():
                dve.wait_ge(small_in, 32)
                nc.vector.tensor_scalar(sp[:, 0, :], ew[:], -1.0, None, ALU.mult).then_inc(sp_step, 1)
                nc.vector.tensor_scalar(sp[:, 4, :], ew[:], 0.0, None, ALU.max).then_inc(sp_step, 1)
                dve.wait_ge(sp_step, 1)
                nc.vector.tensor_tensor(sp[:, 1, :], sp[:, 0, :], ew[:], ALU.min).then_inc(sp_in, 1)

            def softplus_out():
                dve.wait_ge(sp_ln, 1)
                dve.wait_ge(sp_step, 2)
                nc.vector.tensor_tensor(sp[:, 0, :], sp[:, 3, :], sp[:, 4, :], ALU.add).then_inc(sp_step, 1)
                dve.wait_ge(sp_step, 3)
                nc.vector.tensor_scalar(sp[:, 1, :], sp[:, 0, :], 1.0 / SCALE, None, ALU.mult).then_inc(sp_ok, 1)

            def tile_lo_part(t):
                hi, lo, b, psum = tile_place(t)
                if t < 3 * KT:
                    dve.wait_ge(tile_hi, t + 1)
                    nc.vector.scalar_tensor_tensor(lo, psum[:, 0:N], bias[:, b:b + 1], hi.bitcast(F32),
                                                   op0=ALU.add, op1=ALU.subtract).then_inc(tile_lo, 1)
                    return
                pair, is_k = (t - 3 * KT) // 2, t % 2
                turn = pair % 2
                for h in range(2):
                    own, other = rows_of(h)
                    dve.wait_ge(tile_hi, tile_hi_count(t) - 1 + h)
                    hi = (q2, k2_hi)[is_k][own, turn, h, :].bitcast(F32)
                    lo = k2_lo[own, turn, h, :] if is_k else q2[other, turn, h, :]
                    mm = nc.vector.scalar_tensor_tensor(lo, psum[own, 0:N], bias[own, b:b + 1], hi, op0=ALU.add,
                                                        op1=ALU.subtract)
                    if is_k:
                        mm.then_inc(k2_step if h == 0 else k2_read, 1)
                if not is_k:
                    mm.then_inc(tile_lo, 1)

            def k2_other_half(pair):
                turn = pair % 2
                dve.wait_ge(k2_step, pair + 1)
                dve.wait_ge(k2_read, pair + 1)
                for part in (k2_hi, k2_lo):
                    for h in range(2):
                        own, other = rows_of(h)
                        last = nc.vector.tensor_copy(part[other, turn, h, :], part[own, turn, h, :].bitcast(F32))
                last.then_inc(tile_lo, 1)

            def pair_lo_part(pair):
                dve.wait_ge(head_hi, pair + 1)
                nc.vector.tensor_tensor(a_lo[:, pair, :], head_out, a_hi[:, pair, :].bitcast(F32),
                                        ALU.subtract).then_inc(head_lo, 1)

            def build_mask():
                dve.wait_ge(hot_used, ET)
                dve.wait_ge(diag_ok, NT)
                for t in range(NT):
                    nc.vector.tensor_tensor(winner[:, t, :], mask_bank[t][:, 0:N], diag[:, t, :],
                                            ALU.max).then_inc(mask_step, 1)
                dve.wait_ge(mask_step, NT)
                nc.vector.tensor_scalar(cls[:], winner[:].bitcast(I32), 23, 3, ALU.logical_shift_right,
                                        ALU.bitwise_and).then_inc(mask_step, 1)
                nc.vector.tensor_scalar(mask[:], winner[:], 0.0, LOW, ALU.is_equal, ALU.mult).then_inc(mask_step, 1)
                dve.wait_ge(sp_ok, 1)
                for c in range(4):
                    dve.wait_ge(mask_step, NT + 2 + 2 * c)
                    nc.vector.tensor_scalar(pick[:, c % 2], cls[:], float(c), sp[:, 1, c:c + 1], ALU.is_equal,
                                            ALU.mult).then_inc(mask_step, 1)
                    dve.wait_ge(mask_step, NT + 3 + 2 * c)
                    nc.vector.tensor_tensor(mask[:], mask[:], pick[:, c % 2], ALU.add).then_inc(
                        mask_step if c < 3 else mask_ok, 1)

            edge_unit_values(0)
            for k in range(KT):
                dve.wait_ge(h_hi, k + 1)
                nc.vector.tensor_tensor(a_lo[:, k, :], h_bank[k % 3][:, 0:N], a_hi[:, k, :].bitcast(F32),
                                        ALU.subtract).then_inc(h_lo, 1)
                if 0 <= k - HOT_FROM < EG:
                    edge_tile_hot(k - HOT_FROM)
            unit = 1
            for s in range(QK0 + TILES_AHEAD):
                if s < VV0:
                    for _ in range(UNITS_OF_SLAB[s]):
                        edge_unit(unit)
                        unit += 1
                    tile_lo_part(s)
                    if s == 1:
                        softplus_in()
                    if s == 4:
                        softplus_out()
                    if s == VV0 - 1:
                        build_mask()
                elif s < Q0:
                    g, k = (s - VV0) // KS, (s - VV0) % KS
                    if k == KS - 1:
                        for t in range(NT):
                            dve.wait_ge(v2_hi, g * NT + t + 1)
                            pairs = slice(g * PAIRS // GS, (g + 1) * PAIRS // GS)
                            nc.vector.tensor_tensor(
                                v2[:, t, pairs, 1:3, :], v2_bank[g][t][:, :].rearrange("p (a b d) -> p a b d", b=2, d=D),
                                v2[:, t, pairs, 0:4:3, :].bitcast(F32), ALU.subtract).then_inc(v2_lo, 1)
                else:
                    tile_lo_part(s - KT)
                    if s == QK0 + 1:
                        k2_other_half(0)

            def neg_max_part(i, t):
                dve.wait_ge(masked, i * NT + t + 1)
                nc.vector.tensor_scalar(neg_max[:, i % 2, t:t + 1], row_max[:, i % 2, t:t + 1], -SCALE, None,
                                        ALU.mult).then_inc(neg_max_ok, 1)

            for i in range(H + 1):
                if i < H:
                    for t in range(NT):
                        dve.wait_ge(score_done, i * NT + t + 1)
                        if i == 0:
                            dve.wait_ge(mask_ok, 1)
                        nc.vector.tensor_tensor_reduce(
                            out=prob[:, i % 2, t, :], in0=score_bank[t][:, 0:N], in1=mask[:, t, :], scale=1.0,
                            scalar=-3.4e38, op0=ALU.add, op1=ALU.max,
                            accum_out=row_max[:, i % 2, t:t + 1]).then_inc(masked, 1)
                        if t >= 1:
                            neg_max_part(i, t - 1)
                    neg_max_part(i, NT - 1)
                if i >= 1:
                    for m in range(NT):
                        dve.wait_ge(pt_hi_ok, (i - 1) * NT + m + 1)
                        nc.vector.tensor_tensor(pt_lo[:, m, :], pt_bank[m][:, 0:N], pt_hi[:, m, :].bitcast(F32),
                                                ALU.subtract).then_inc(pt_lo_ok, 1)
                if i == H - TILES_AHEAD:
                    k2_other_half(PAIRS - 1)
                if i < H:
                    for t in range(NT):
                        dve.wait_ge(exp_done, i * NT + t + 1)
                        nc.vector.reciprocal(row_inv[:, i % 2, t:t + 1], row_sum[:, i % 2, t:t + 1]).then_inc(inv_ok, 1)
                if H - TILES_AHEAD <= i < H:
                    for t in range(1, NT):
                        dve.wait_ge(inv_ok, i * NT + t + 1)
                        nc.vector.tensor_scalar(prob[:, i % 2, t, :], prob[:, i % 2, t, :],
                                                row_inv[:, i % 2, t:t + 1], None, ALU.mult).then_inc(prob_ok, 1)
                if i % 2 == 1 and i < H - TILES_AHEAD:
                    k2_other_half((i + 1) // 2)
                if i < H - TILES_AHEAD:
                    tile_lo_part(3 * KT + TILES_AHEAD + i)
                if i == H - 1:
                    pair_lo_part(PAIRS - 2)
                if i >= 1:
                    own, _ = rows_of(i - 1)
                    dve.wait_ge(half_ok, i)
                    if i >= 3:
                        dve.wait_ge(head_lo, (i - 1) // 2)
                    nc.vector.tensor_tensor(head_out[own, :], head_bank[own, 0:N], half_sum[own, :],
                                            ALU.add).then_inc(head_sum, 1)
            pair_lo_part(PAIRS - 1)
            dve.wait_ge(y_ok, NT)
            for g in range(GS):
                for t in range(NT):
                    dve.wait_ge(out_done, g * NT + t + 1)
                    part = slice(g * HALF, (g + 1) * HALF)
                    nc.vector.tensor_tensor(y[:, t, part], out_bank[g][t][:, :], y[:, t, part],
                                            ALU.add).then_inc(out_ok, 1)

        @block.tensor
        def _(pe):
            def products(psum, w, a, first, last):
                nc.tensor.matmul(psum, w[0], a[0], start=first, stop=False)
                nc.tensor.matmul(psum, w[0], a[1], start=False, stop=False)
                return nc.tensor.matmul(psum, w[1], a[0], start=False, stop=last)

            def keys(g):
                for t in tiles_of(g):
                    mm = nc.tensor.matmul(key_bank[g % 2][:, (t % EG) * P:(t % EG + 1) * P],
                                          select[:, t:t + 1].to_broadcast([P, P]), rows[:], start=True, stop=True)
                mm.then_inc(keys_done, 1)

            def edge_unit(g):
                for t in tiles_of(g):
                    pe.wait_ge(hot_ok, 2 * (t + 1))
                    for n in range(NT):
                        mm = nc.tensor.matmul(mask_bank[n][:, 0:N], hot_src[:, t % HOTS, n * P:(n + 1) * P],
                                              hot_dst[:, t % HOTS, :], start=(t == 0), stop=(t == ET - 1))
                    mm.then_inc(hot_used, 1)
                if g + 2 < GROUPS:
                    pe.wait_ge(later_ok, tiles_of(g)[-1] + 1)
                    keys(g + 2)

            def split_slab(s):
                pe.wait_ge(slab_lo, s + 1)
                return split_place(s)

            def tile(t, a_h, a_l, ks=range(KT)):
                if t == 0 and ks[-1] < KT // 2:
                    pe.wait_ge(half_lo, 1)
                    hi, lo = split_place(0)
                else:
                    hi, lo = split_slab(slab_of(t))
                if t >= 3 * KT + 5:
                    if t % 2 == 0:
                        pe.wait_ge(k2_read, t // 2 - 3 * KT // 2)
                    else:
                        pe.wait_ge(tile_lo, t)
                elif t >= 2:
                    pe.wait_ge(tile_lo, t - 1)
                psum = tile_place(t)[3]
                for k in ks:
                    if t == 0:
                        pe.wait_ge(h_lo, k + 1)
                    c = slice(k * P, (k + 1) * P)
                    mm = products(psum[:, 0:N], (hi[:, c], lo[:, c]), (a_h[:, k, :], a_l[:, k, :]), k == 0, k == KT - 1)
                if k == KT - 1:
                    mm.then_inc(slab_used, 1)

            def moving(s, base, a_h, a_l, banks, done):
                hi, lo = split_slab(s)
                g, part = (s - base) // KS, (s - base) % KS
                for n in range(NT):
                    m = slice(n * P, (n + 1) * P)
                    for b in range(GS):
                        k, c = part * GS + b, slice(b * HALF, (b + 1) * HALF)
                        mm = products(banks[g][n][:, :], (a_h[:, k, m], a_l[:, k, m]), (hi[:, c], lo[:, c]),
                                      k == 0, k == KT - 1)
                    if n == NT - 1:
                        mm.then_inc(slab_used, 1)
                    elif part == KS - 1:
                        mm.then_inc(done, 1)

            pe.wait_ge(rows_ok, 1)
            pe.wait_ge(select_ok, 1)
            keys(0)
            pe.wait_ge(h_ok, NT)
            pe.wait_ge(ident_ok, 1)
            for k in range(KT):
                if k == HALF // P:
                    pe.wait_ge(h_ok, NT + 1)
                if k >= 3:
                    pe.wait_ge(h_lo, k - 2)
                for t in range(NT):
                    mm = nc.tensor.transpose(h_bank[k % 3][:, t * P:(t + 1) * P], x_sb[:, t, k * P:(k + 1) * P], ident[:])
                mm.then_inc(h_turned, 1)
                if k >= 2:
                    tile(0, a_hi, a_lo, [k - 2])
            tile(0, a_hi, a_lo, range(KT - 2, KT))
            keys(1)
            edge_unit(0)
            unit = 1
            for t in range(KT):
                if t >= 1:
                    tile(t, a_hi, a_lo)
                for _ in range(UNITS_OF_SLAB[t]):
                    edge_unit(unit)
                    unit += 1
            for s in range(VV0, Q0):
                if s == VV0 + KS:
                    pe.wait_ge(mask_step, NT)
                if s - VV0 < KS:
                    pe.wait_ge(tile_lo, (s - VV0 + 1) * GS)
                moving(s, VV0, b_hi, b_lo, v2_bank, v2_done)
            for t in range(KT, 3 * KT):
                tile(t, a_hi, a_lo)

            def pair_tile(t):
                if t % 2 == 0:
                    tile(t, b_hi, b_lo)
                else:
                    tile(t, c_hi, c_lo)

            def scores(h):
                turn = h // 2 % 2
                if h % 2 == 0:
                    pe.wait_ge(tile_lo, 3 * KT + h + 2)
                for n in range(NT):
                    if h >= 1:
                        pe.wait_ge(masked, (h - 1) * NT + n + 1)
                    m = slice(n * P, (n + 1) * P)
                    nc.tensor.matmul(score_bank[n][:, 0:N], q2[:, turn, h % 2, m], k2_hi[:, turn, h % 2, :],
                                     start=True, stop=False)
                    nc.tensor.matmul(score_bank[n][:, 0:N], q2[:, turn, h % 2, m], k2_lo[:, turn, h % 2, :],
                                     start=False, stop=True).then_inc(score_done, 1)

            def turn_probs(h):
                pe.wait_ge(prob_ok, (h + 1) * NT)
                for m in range(NT):
                    if h >= 1:
                        pe.wait_ge(pt_lo_ok, (h - 1) * NT + m + 1)
                    for n in range(NT):
                        mm = nc.tensor.transpose(pt_bank[m][:, n * P:(n + 1) * P],
                                                 prob[:, h % 2, n, m * P:(m + 1) * P], ident[:])
                    mm.then_inc(pt_done, 1)

            def heads_values(h):
                pair = h // 2
                if h >= 1:
                    pe.wait_ge(head_sum, h)
                else:
                    pe.wait_ge(k2_read, 2)
                for m in range(NT):
                    pe.wait_ge(pt_lo_ok, h * NT + m + 1)
                    w = v2[:, m, pair, 2 * (h % 2):2 * (h % 2) + 2, :]
                    nc.tensor.matmul(head_bank[:, 0:N], w, pt_hi[:, m, :], start=(m == 0), stop=False)
                    mm = nc.tensor.matmul(head_bank[:, 0:N], w, pt_lo[:, m, :], start=False, stop=(m == NT - 1))
                mm.then_inc(head_done, 1)

            def out_part(g, n, ks):
                m = slice(n * P, (n + 1) * P)
                for k in ks:
                    s, b = O0 + g * KS + k // GS, k % GS
                    pe.wait_ge(head_lo, k + 1)
                    hi, lo = split_slab(s)
                    c = slice(b * HALF, (b + 1) * HALF)
                    mm = products(out_bank[g][n][:, :], (a_hi[:, k, m], a_lo[:, k, m]), (hi[:, c], lo[:, c]),
                                  k == 0, k == KT - 1)
                if k == KT - 1:
                    mm.then_inc(out_done, 1)

            pe.wait_ge(v2_lo, GS * NT)
            for t in range(TILES_AHEAD):
                pair_tile(3 * KT + t)
            for i in range(H + 1):
                if i < H:
                    scores(i)
                if i == H:
                    out_part(0, 2, range(0, KT - 2))
                if i >= 1:
                    turn_probs(i - 1)
                if i < H - TILES_AHEAD:
                    pair_tile(3 * KT + TILES_AHEAD + i)
                elif i == H - 3:
                    pe.wait_ge(k2_read, PAIRS)
                    out_part(0, 0, range(0, 4))
                elif i == H - 2:
                    out_part(0, 0, range(4, 5))
                elif i == H - 1:
                    out_part(0, 0, range(5, KT - 2))
                    pe.wait_ge(masked, H * NT)
                    out_part(0, 1, range(0, KT - 2))
                else:
                    for n in range(NT):
                        out_part(0, n, [KT - 2])
                if i >= 1:
                    heads_values(i - 1)
            out_part(1, 0, range(0, KT - 1))
            for n in range(NT):
                out_part(0, n, [KT - 1])
            out_part(1, 0, [KT - 1])
            out_part(1, 1, range(KT))
            out_part(1, 2, range(KT))


def kernel(x, src, dst, edge_type_5, L0_gnn_edge_type_weights, L0_gnn_wq, L0_gnn_bq, L0_gnn_wk, L0_gnn_bk,
           L0_gnn_wv, L0_gnn_bv, L0_gnn_wiq, L0_gnn_biq, L0_gnn_wik, L0_gnn_bik, L0_gnn_wiv, L0_gnn_biv,
           L0_gnn_wo, L0_gnn_bo):
    import concourse.bacc as bacc
    from concourse.bass_utils import run_bass_kernel_spmd

    def stay(w):
        return np.asarray(w).reshape(KT, P, KT, P).transpose(0, 3, 2, 1).reshape(KT, P, F)

    def move(w):
        return np.asarray(w).reshape(GS, HALF, KS, GS, P).transpose(0, 2, 4, 3, 1).reshape(KT, P, F)

    second = np.stack([stay(L0_gnn_wiq), stay(L0_gnn_wik)], axis=1).reshape(2 * KT, P, F)
    slabs = np.concatenate([stay(L0_gnn_wv), move(L0_gnn_wiv), stay(L0_gnn_wq), stay(L0_gnn_wk), second,
                            move(L0_gnn_wo)])
    edges = [np.asarray(a).reshape(ET, P) for a in (src, dst, edge_type_5)]
    rows = np.zeros((P, P), edges[0].dtype)
    rows[0:ET], rows[DST_ROW:DST_ROW + ET] = edges[0], edges[1]
    biases = np.concatenate([np.asarray(b).reshape(KT, P) for b in (
        L0_gnn_bq, L0_gnn_bk, L0_gnn_bv, L0_gnn_biq, L0_gnn_bik, L0_gnn_biv)]).T
    arrays = {
        "in_slabs": slabs, "in_x": np.asarray(x), "in_edge_cols": np.stack(edges).transpose(2, 0, 1),
        "in_edge_rows": rows, "in_edge_weights": np.asarray(L0_gnn_edge_type_weights), "in_biases": biases,
        "in_bo": np.asarray(L0_gnn_bo),
    }
    arrays = {name: np.ascontiguousarray(a) for name, a in arrays.items()}
    nc = bacc.Bacc("TRN2", target_bir_lowering=False, num_devices=1)
    args = [nc.dram_tensor(name, a.shape, mybir.dt.from_np(a.dtype), kind="ExternalInput").ap()
            for name, a in arrays.items()]
    out = nc.dram_tensor("out_y", (N, F), F32, kind="ExternalOutput").ap()
    gat_kernel(nc, *args, out)
    return run_bass_kernel_spmd(nc, [arrays], core_ids=[0]).results[0]["out_y"]
```

```python
from contextlib import ExitStack

import numpy as np
import concourse.bass as bass
from concourse import mybir

F32 = mybir.dt.float32
F32R = mybir.dt.float32r
F16 = mybir.dt.float16
BF16 = mybir.dt.bfloat16
I32 = mybir.dt.int32
ALU = mybir.AluOpType
ACT = mybir.ActivationFunctionType

P = 128
N = 384
F = 1024
H = 16
D = F // H
NT = N // P
KT = F // P
PAIRS = H // 2
E = 6528
ET = E // P
EG = 4
GROUPS = -(-ET // EG)
DST_ROW = 64
NW = 3 + 3 + 1
SLABS = NW * KT
HALF = 512
GS = F // HALF
KS = KT // GS
RAW = 3
RING = 4
AHEAD = RING - 1
HOTS = 2 * EG
EPS = 1e-5
LOW = -3.0e38
SCALE = 1.0 / float(np.sqrt(D))
EXP0 = 24
assert SCALE == 0.125 and H * D == F and ET * P == E and EXP0 + 4 * ET < 254

V0, VV0, Q0, K0, QK0, O0 = 0, KT, 2 * KT, 3 * KT, 4 * KT, 6 * KT
BQ, BK, BV, BIQ, BIK, BIV = (n * KT for n in range(6))
WARM = 13
HOT_FROM = 2
UNITS_OF_SLAB = [0, 1, 2, 2, 2, 1, 2, 2]
PAIRS_BY_POOL = PAIRS - 2
TILES_AHEAD = 3
assert 1 + sum(UNITS_OF_SLAB) == GROUPS


def tiles_of(group):
    return range(group * EG, min((group + 1) * EG, ET))


def gat_kernel(nc, slabs, x, edge_cols, edge_rows, edge_weights, biases, bo, out):
    with ExitStack() as ctx:
        def sb(name, shape, dt):
            return ctx.enter_context(nc.sbuf_tensor(name, shape, dt))

        def sem(name):
            return ctx.enter_context(nc.semaphore(name))

        x_sb = sb("x_sb", [P, NT, F], F32)
        a_hi = sb("a_hi", [P, KT, N], F32R)
        a_lo = sb("a_lo", [P, KT, N], F32R)
        b_hi = sb("b_hi", [P, KT, N], F32R)
        b_lo = sb("b_lo", [P, KT, N], F32R)
        c_hi = sb("c_hi", [P, KT, N], F32R)
        c_lo = sb("c_lo", [P, KT, N], F32R)
        v2 = sb("v2", [P, NT, PAIRS, 4, D], F32R)
        raw = sb("raw", [P, RAW, F], F32)
        w_hi = sb("w_hi", [P, RING, F], F32R)
        w_lo = sb("w_lo", [P, RING, F], F32R)
        q2 = sb("q2", [P, 2, 2, N], F32R)
        k2_hi = sb("k2_hi", [P, 2, 2, N], F32R)
        k2_lo = sb("k2_lo", [P, 2, 2, N], F32R)
        work = sb("work", [P, NT * N + N], F32)
        prob = sb("prob", [P, 2, NT, N], F32)
        pt_hi = sb("pt_hi", [P, NT, N], F32R)
        pt_lo = sb("pt_lo", [P, NT, N], F32R)
        work2 = sb("work2", [P, NT * N + N], F32)
        bias = sb("bias", [P, 6 * KT], F32)
        cols_i = sb("cols_i", [P, 3, ET], I32)
        cols = sb("cols", [P, 2, ET], F32)
        rows_i = sb("rows_i", [P, P], I32)
        rows = sb("rows", [P, P], F16)
        key = sb("key", [P, ET], F32)
        later = sb("later", [P, ET], F32)
        junk = sb("junk", [P, 2, P], BF16)
        expo = sb("expo", [P, ET], F32)
        live_expo = sb("live_expo", [P, ET], F32)
        value_bits = sb("value_bits", [P, ET], I32)
        type3 = sb("type3", [P, ET], I32)
        cls_e = sb("cls_e", [P, ET], I32)
        tile_expo = sb("tile_expo", [P, ET], F32)
        iota = sb("iota", [P, N], F16)
        select = sb("select", [P, ET], F16)
        above = sb("above", [P, P], F16)
        ident = sb("ident", [P, P], F32)
        ew = sb("ew", [P, 4], F32)
        sp = sb("sp", [P, 5, 4], F32)
        stats = sb("stats", [P, NT, 2, 6], F32)
        mean_var = sb("mean_var", [P, NT, 2], F32)
        var_eps = sb("var_eps", [P, NT], F32)
        minus_half = sb("minus_half", [P, NT], F32)
        rstd = sb("rstd", [P, NT], F32)
        shift = sb("shift", [P, NT], F32)
        row_max = sb("row_max", [P, 2, NT], F32)
        neg_max = sb("neg_max", [P, 2, NT], F32)
        row_sum = sb("row_sum", [P, 2, NT], F32)
        row_inv = sb("row_inv", [P, 2, NT], F32)
        y = x_sb
        assert HOTS * N * 2 == (NT + 1) * N * 4
        hot_src = work[:, :].bitcast(BF16).rearrange("p (r n) -> p r n", n=N)
        mask = work[:, 0:NT * N].rearrange("p (t n) -> p t n", n=N)
        half_sum = work[:, NT * N:(NT + 1) * N]
        hot_dst = work2[:, :].bitcast(BF16).rearrange("p (r n) -> p r n", n=N)
        bo_sb = work2[:, 0:F]
        head_out = work2[:, F:F + N]
        diag = prob[:, 0]
        pick = prob
        winner = x_sb[:, 0:2, :].rearrange("p a b -> p (a b)")[:, 0:NT * N].rearrange("p (t n) -> p t n", n=N)
        cls = x_sb[:, 1:3, :].rearrange("p a b -> p (a b)")[:, 2 * F - NT * N:].bitcast(I32).rearrange("p (t n) -> p t n", n=N)

        bank = [ctx.enter_context(nc.psum_tensor(f"bank{i}", [P, HALF], F32)) for i in range(8)]
        mask_bank = bank[0:3]
        key_bank = bank[6:8]
        h_bank = [bank[5], bank[4], bank[7]]
        tile_bank = bank[3:5]
        v2_bank = [bank[5:8], bank[0:3]]
        score_bank = bank[0:3]
        pt_bank = bank[5:8]
        pair_bank = bank[3]
        head_bank = bank[4]
        cut = HALF + HALF // 2
        out_pieces = [(0, n, slice(0, HALF), bank[b][:, :]) for n, b in enumerate((3, 0, 1))]
        out_pieces += [(1, n, slice(HALF, F), bank[b][:, :]) for n, b in enumerate((2, 5))]
        out_pieces += [(1, 2, slice(HALF, cut), bank[6][:, 0:cut - HALF]), (1, 2, slice(cut, F), bank[7][:, 0:F - cut])]

        edges_in, small_in, y_in = sem("edges_in"), sem("small_in"), sem("y_in")
        x_half_in = sem("x_half_in")
        x_in = [sem(f"x_in{t}") for t in range(NT)]
        slab_in = [sem(f"slab_in{r}") for r in range(RAW)]
        const_step, iota_ok, select_ok, above_ok = sem("const_step"), sem("iota_ok"), sem("select_ok"), sem("above_ok")
        tile_expo_ok, ident_ok, diag_ok = sem("tile_expo_ok"), sem("ident_ok"), sem("diag_ok")
        edge_step, rows_ok, keys_done, later_ok, value_ok = (
            sem("edge_step"), sem("rows_ok"), sem("keys_done"), sem("later_ok"), sem("value_ok"))
        expo_live = sem("expo_live")
        hot_ok, hot_used = sem("hot_ok"), sem("hot_used")
        sp_step, sp_in, sp_exp, sp_ln, sp_ok = sem("sp_step"), sem("sp_in"), sem("sp_exp"), sem("sp_ln"), sem("sp_ok")
        mask_step, mask_ok = sem("mask_step"), sem("mask_ok")
        stats_step, stats_agg, var_ok, rstd_ok, shift_ok, h_ok = (
            sem("stats_step"), sem("stats_agg"), sem("var_ok"), sem("rstd_ok"), sem("shift_ok"), sem("h_ok"))
        h_step, h_last_ok = sem("h_step"), sem("h_last_ok")
        h_turned, h_hi, h_lo = sem("h_turned"), sem("h_hi"), sem("h_lo")
        half_hi, half_lo = sem("half_hi"), sem("half_lo")
        slab_hi, slab_lo, slab_used = sem("slab_hi"), sem("slab_lo"), sem("slab_used")
        tile_hi, tile_lo, k2_step = sem("tile_hi"), sem("tile_lo"), sem("k2_step")
        k2_read = sem("k2_read")
        v2_done, v2_hi, v2_lo = sem("v2_done"), sem("v2_hi"), sem("v2_lo")
        score_done, masked, neg_max_ok = sem("score_done"), sem("masked"), sem("neg_max_ok")
        exp_done, inv_ok, prob_ok = sem("exp_done"), sem("inv_ok"), sem("prob_ok")
        pt_done, pt_hi_ok, pt_lo_ok = sem("pt_done"), sem("pt_hi_ok"), sem("pt_lo_ok")
        head_done, half_ok, head_sum, head_hi, head_lo = (
            sem("head_done"), sem("half_ok"), sem("head_sum"), sem("head_hi"), sem("head_lo"))
        y_ok, out_done, out_ok, stored = sem("y_ok"), sem("out_done"), sem("out_ok"), sem("stored")

        block = ctx.enter_context(nc.Block())

        def tile_place(t):
            stage, j = t // KT, t % KT
            if stage < 3:
                hi, lo, b = [(b_hi, b_lo, BV), (b_hi, b_lo, BQ), (c_hi, c_lo, BK)][stage]
                return hi[:, j, :], lo[:, j, :], b + j, tile_bank[t % 2]
            pair, which = (t - 3 * KT) // 2, t % 2
            return None, None, (BIQ, BIK)[which] + pair, bank[4] if t - 3 * KT in (1, 3) else pair_bank

        def tile_hi_count(t):
            return t + 1 + max(0, t + 1 - 3 * KT)

        def split_place(s):
            j = s - O0 - KS
            if j < 0:
                return w_hi[:, s % RING, :], w_lo[:, s % RING, :]
            hi, lo = (b_hi, b_lo) if j < 3 else (c_hi, c_lo)
            part = slice(j % 3 * F, (j % 3 + 1) * F)
            return tuple(a[:, :, :].rearrange("p k n -> p (k n)")[:, part] for a in (hi, lo))

        def wait_split_place(eng, s):
            if s >= O0 + KS:
                eng.wait_ge(slab_used, O0)
            elif s >= RING:
                eng.wait_ge(slab_used, s - RING + 1)

        def slabs_of_step(i):
            first = QK0 + TILES_AHEAD + AHEAD + i
            return range(first + (i == H), min(first + 1 + (i >= H - 1), SLABS))

        def slab_of(t):
            return t if t < KT else t + KT

        def rows_of(h):
            own = (h % 2) * D
            return slice(own, own + D), slice(D - own, 2 * D - own)

        @block.sync
        def _(sp_eng):
            sp_eng.dma_start(rows_i[:], edge_rows).then_inc(edges_in, 16)
            sp_eng.dma_start(cols_i[:], edge_cols).then_inc(edges_in, 16)
            sp_eng.dma_start(x_sb[:, 0, 0:HALF], x[0:P, 0:HALF]).then_inc(x_half_in, 16)
            sp_eng.dma_start(x_sb[:, 0, HALF:F], x[0:P, HALF:F]).then_inc(x_in[0], 16)
            for t in range(1, NT):
                sp_eng.dma_start(x_sb[:, t, :], x[t * P:(t + 1) * P, :]).then_inc(x_in[t], 16)
            for s in range(RAW):
                sp_eng.dma_start(raw[:, s, :], slabs[s]).then_inc(slab_in[s], 16)
                if s == 0:
                    sp_eng.dma_start(bias[:], biases).then_inc(small_in, 16)
                    sp_eng.dma_start(ew[:], edge_weights.rearrange("(a n) -> a n", a=1).to_broadcast([P, 4])).then_inc(small_in, 16)

            def load_slab(s, turn):
                sp_eng.wait_ge(slab_lo, s - RAW + 1)
                sp_eng.dma_start(raw[:, turn, :], slabs[bass.ds(s, 1)].rearrange("s p f -> p (s f)")).then_inc(
                    slab_in[turn], 16)

            def load_slabs(first, last):
                with sp_eng.Fori(first, last, RAW) as s:
                    for turn in range(RAW):
                        load_slab(s + turn, turn)

            assert (Q0 - 1) % RAW == 0
            load_slabs(RAW, Q0 + RAW - 1)
            sp_eng.wait_ge(h_turned, KT)
            sp_eng.wait_ge(mask_ok, 1)
            for t in range(NT):
                sp_eng.dma_start(y[:, t, :], x[t * P:(t + 1) * P, :]).then_inc(y_in, 16)
            sp_eng.dma_start(bo_sb, bo.rearrange("(a n) -> a n", a=1).to_broadcast([P, F])).then_inc(y_in, 16)
            load_slabs(Q0 + RAW - 1, SLABS - SLABS % RAW)
            for s in range(SLABS - SLABS % RAW, SLABS):
                load_slab(s, s % RAW)
            for i, (_, n, cols_out, _) in enumerate(out_pieces):
                sp_eng.wait_ge(out_ok, i + 1)
                sp_eng.dma_start(out[n * P:(n + 1) * P, cols_out], y[:, n, cols_out]).then_inc(stored, 16)
            sp_eng.wait_ge(stored, 16 * len(out_pieces))

        @block.gpsimd
        def _(pool):
            nc.gpsimd.iota(iota[:], pattern=[[1, N]], base=0, channel_multiplier=0,
                           allow_small_or_imprecise_dtypes=True).then_inc(iota_ok, 1)
            nc.gpsimd.memset(select[:], 0.0).then_inc(const_step, 1)
            nc.gpsimd.memset(above[:], 1.0).then_inc(const_step, 1)
            nc.gpsimd.memset(ident[:], 0.0).then_inc(const_step, 1)
            nc.gpsimd.memset(diag[:], 0.0).then_inc(const_step, 1)
            nc.gpsimd.memset(minus_half[:], -0.5).then_inc(const_step, 1)
            nc.gpsimd.iota(tile_expo[:], pattern=[[4, ET]], base=EXP0, channel_multiplier=0,
                           allow_small_or_imprecise_dtypes=True).then_inc(tile_expo_ok, 1)
            pool.wait_ge(const_step, 5)
            nc.gpsimd.affine_select(out=select[:], in_=select[:], compare_op=ALU.not_equal, fill=float(N),
                                    base=0, pattern=[[-1, ET]], channel_multiplier=1).then_inc(const_step, 1)
            pool.wait_ge(const_step, 6)
            nc.gpsimd.affine_select(out=select[:], in_=select[:], compare_op=ALU.not_equal, fill=1.0,
                                    base=-DST_ROW, pattern=[[-1, ET]], channel_multiplier=1).then_inc(select_ok, 1)
            nc.gpsimd.affine_select(out=above[:], in_=above[:], compare_op=ALU.is_gt, fill=0.0,
                                    base=0, pattern=[[1, P]], channel_multiplier=-1).then_inc(above_ok, 1)
            nc.gpsimd.affine_select(out=ident[:], in_=ident[:], compare_op=ALU.not_equal, fill=1.0,
                                    base=0, pattern=[[-1, P]], channel_multiplier=1).then_inc(ident_ok, 1)
            for t in range(NT):
                nc.gpsimd.affine_select(out=diag[:, t, :], in_=diag[:, t, :], compare_op=ALU.not_equal,
                                        fill=2.0 ** (EXP0 - 1 - 127), base=t * P, pattern=[[-1, N]],
                                        channel_multiplier=1).then_inc(diag_ok, 1)
            for t in range(NT):
                pool.wait_ge(var_ok, t + 1)
                nc.gpsimd.tensor_tensor(rstd[:, t:t + 1], var_eps[:, t:t + 1], minus_half[:, 0:1],
                                        ALU.pow).then_inc(rstd_ok, 1)

            def split_lo(s, turn=None):
                turn = s if turn is None else turn
                pool.wait_ge(slab_hi, s + 1)
                hi, lo = split_place(turn)
                nc.gpsimd.tensor_tensor(lo, raw[:, turn % RAW, :], hi.bitcast(F32), ALU.subtract).then_inc(slab_lo, 1)

            def pair_lo_part(pair):
                pool.wait_ge(head_hi, pair + 1)
                nc.gpsimd.tensor_tensor(a_lo[:, pair, :], head_out, a_hi[:, pair, :].bitcast(F32),
                                        ALU.subtract).then_inc(head_lo, 1)

            for b in range(2):
                half = slice(b * HALF, (b + 1) * HALF)
                pool.wait_ge((half_hi, slab_hi)[b], 1)
                nc.gpsimd.tensor_tensor(w_lo[:, 0, half], raw[:, 0, half], w_hi[:, 0, half].bitcast(F32),
                                        ALU.subtract).then_inc((half_lo, slab_lo)[b], 1)
            with pool.Fori(1, 1 + 2 * RAW * RING, RAW * RING) as s:
                for turn in range(RAW * RING):
                    split_lo(s + turn, 1 + turn)
            pool.wait_ge(y_in, 16 * (NT + 1))
            for t in range(NT):
                nc.gpsimd.tensor_tensor(y[:, t, :], y[:, t, :], bo_sb, ALU.add).then_inc(y_ok, 1)
            for s in range(1 + 2 * RAW * RING, QK0 + TILES_AHEAD + AHEAD):
                split_lo(s)
            for i in range(H + 1):
                if i >= 3 and i % 2 == 1 and (i - 3) // 2 < PAIRS_BY_POOL:
                    pair_lo_part((i - 3) // 2)
                if i < H:
                    for t in range(NT if i < H - TILES_AHEAD else 1):
                        pool.wait_ge(inv_ok, i * NT + t + 1)
                        nc.gpsimd.tensor_scalar(prob[:, i % 2, t, :], prob[:, i % 2, t, :],
                                                row_inv[:, i % 2, t:t + 1], 1.0, ALU.mult,
                                                ALU.mult).then_inc(prob_ok, 1)
                for s in slabs_of_step(i):
                    split_lo(s)

        @block.scalar
        def _(act):
            def split_hi(s):
                act.wait_ge(slab_in[s % RAW], 16 * (s // RAW + 1))
                wait_split_place(act, s)
                nc.scalar.activation(split_place(s)[0], raw[:, s % RAW, :], ACT.Copy).then_inc(slab_hi, 1)

            def tile_hi_part(t):
                hi, _, b, psum = tile_place(t)
                act.wait_ge(slab_used, slab_of(t) + 1)
                if t < 3 * KT:
                    nc.scalar.activation(hi, psum[:, 0:N], ACT.Identity, bias=bias[:, b:b + 1]).then_inc(tile_hi, 1)
                    return
                turn, dst = (t - 3 * KT) // 2 % 2, (q2, k2_hi)[t % 2]
                for h in range(2):
                    own, _ = rows_of(h)
                    nc.scalar.activation(dst[own, turn, h, :], psum[own, 0:N], ACT.Identity,
                                         bias=bias[own, b:b + 1]).then_inc(tile_hi, 1)

            def first_slab_hi(b):
                half = slice(b * HALF, (b + 1) * HALF)
                act.wait_ge(slab_in[0], 16)
                nc.scalar.activation(w_hi[:, 0, half], raw[:, 0, half], ACT.Copy).then_inc((half_hi, slab_hi)[b], 1)

            for t in range(NT):
                if t == NT - 1:
                    first_slab_hi(0)
                act.wait_ge(shift_ok, t + 1)
                part = slice(0, F) if t < NT - 1 else slice(0, HALF)
                nc.scalar.activation(x_sb[:, t, part], x_sb[:, t, part], ACT.Relu, scale=rstd[:, t:t + 1],
                                     bias=shift[:, t:t + 1]).then_inc(h_ok, 1)
            for k in range(KT):
                act.wait_ge(h_turned, k + 1)
                nc.scalar.activation(a_hi[:, k, :], h_bank[k % 3][:, 0:N], ACT.Copy).then_inc(h_hi, 1)
                if k == 0:
                    first_slab_hi(1)
            for s in range(1, AHEAD):
                split_hi(s)
            act.wait_ge(small_in, 32)
            for s in range(QK0 + TILES_AHEAD):
                split_hi(s + AHEAD)
                if s < VV0:
                    tile_hi_part(s)
                    if s == 2:
                        act.wait_ge(sp_in, 1)
                        nc.scalar.activation(sp[:, 2, :], sp[:, 1, :], ACT.Exp).then_inc(sp_exp, 1)
                        act.wait_ge(sp_exp, 1)
                        nc.scalar.activation(sp[:, 3, :], sp[:, 2, :], ACT.Ln, bias=1.0).then_inc(sp_ln, 1)
                        act.wait_ge(sp_ln, 1)
                        nc.scalar.activation(sp[:, 2, :], sp[:, 1, :], ACT.Exp).then_inc(sp_exp, 1)
                elif s < Q0:
                    g, k = (s - VV0) // KS, (s - VV0) % KS
                    if k == KS - 1:
                        for t in range(NT):
                            if t < NT - 1:
                                act.wait_ge(v2_done, g * (NT - 1) + t + 1)
                            else:
                                act.wait_ge(slab_used, s + 1)
                            pairs = PAIRS // GS
                            nc.scalar.activation(
                                v2[:, t, g * pairs:(g + 1) * pairs, 0:4:3, :],
                                v2_bank[g][t][:, :].rearrange("p (a b d) -> p a b d", b=2, d=D),
                                ACT.Copy).then_inc(v2_hi, 1)
                else:
                    tile_hi_part(s - KT)

            def pair_hi_part(pair):
                act.wait_ge(head_sum, 2 * pair + 2)
                nc.scalar.activation(a_hi[:, pair, :], head_out, ACT.Copy).then_inc(head_hi, 1)

            for i in range(H + 1):
                if i >= 3 and i % 2 == 1:
                    pair_hi_part((i - 3) // 2)
                if i >= 1:
                    for m in range(NT):
                        act.wait_ge(pt_done, (i - 1) * NT + m + 1)
                        nc.scalar.activation(pt_hi[:, m, :], pt_bank[m][:, 0:N], ACT.Copy).then_inc(pt_hi_ok, 1)
                if i < H:
                    for t in range(NT):
                        act.wait_ge(neg_max_ok, i * NT + t + 1)
                        nc.scalar.activation(prob[:, i % 2, t, :], prob[:, i % 2, t, :], ACT.Exp, scale=SCALE,
                                             bias=neg_max[:, i % 2, t:t + 1],
                                             accum_out=row_sum[:, i % 2, t:t + 1]).then_inc(exp_done, 1)
                for s in slabs_of_step(i):
                    split_hi(s)
                if i < H - TILES_AHEAD:
                    tile_hi_part(3 * KT + TILES_AHEAD + i)
                if i >= 1:
                    own, other = rows_of(i - 1)
                    act.wait_ge(head_done, i)
                    b = BIV + (i - 1) // 2
                    nc.scalar.activation(half_sum[own, :], head_bank[other, 0:N], ACT.Identity,
                                         bias=bias[own, b:b + 1]).then_inc(half_ok, 1)
            pair_hi_part(PAIRS - 1)

        @block.vector
        def _(dve):
            dve.wait_ge(edges_in, 32)
            nc.vector.tensor_copy(rows[:], rows_i[:]).then_inc(rows_ok, 1)
            nc.vector.tensor_copy(cols[:], cols_i[:, 0:2, :]).then_inc(edge_step, 1)
            nc.vector.tensor_scalar(type3[:], cols_i[:, 2, :], 3, None, ALU.add).then_inc(edge_step, 1)
            dve.wait_ge(edge_step, 2)
            nc.vector.scalar_tensor_tensor(key[:], cols[:, 0, :], float(N), cols[:, 1, :],
                                           op0=ALU.mult, op1=ALU.add).then_inc(edge_step, 1)
            nc.vector.tensor_scalar(cls_e[:], type3[:], 3, None, ALU.bitwise_and).then_inc(edge_step, 1)
            dve.wait_ge(tile_expo_ok, 1)
            dve.wait_ge(edge_step, 4)
            nc.vector.tensor_tensor(expo[:], cls_e[:], tile_expo[:], ALU.add).then_inc(edge_step, 1)

            def shift_part(t):
                dve.wait_ge(rstd_ok, t + 1)
                nc.vector.scalar_tensor_tensor(shift[:, t:t + 1], mean_var[:, t, 0:1], -1.0, rstd[:, t:t + 1],
                                               op0=ALU.mult, op1=ALU.mult).then_inc(shift_ok, 1)

            def edge_unit_later(g, tiles):
                dve.wait_ge(keys_done, g + 1)
                dve.wait_ge(above_ok, 1)
                for t in tiles:
                    if t >= 2:
                        dve.wait_ge(later_ok, t - 1)
                    nc.vector.scalar_tensor_tensor(
                        junk[:, t % 2, :], key_bank[g % 2][:, (t % EG) * P:(t % EG + 1) * P], key[:, t:t + 1], above[:],
                        op0=ALU.is_equal, op1=ALU.mult, accum_out=later[:, t:t + 1]).then_inc(later_ok, 1)

            def edge_unit_values(g):
                tiles = tiles_of(g)
                a, b = tiles[0], tiles[-1] + 1
                dve.wait_ge(later_ok, b)
                nc.vector.scalar_tensor_tensor(live_expo[:, a:b], later[:, a:b], 0.0, expo[:, a:b],
                                               op0=ALU.is_equal, op1=ALU.mult).then_inc(expo_live, 1)
                dve.wait_ge(expo_live, g + 1)
                nc.vector.tensor_scalar(value_bits[:, a:b], live_expo[:, a:b], float(1 << 23), None,
                                        ALU.mult).then_inc(value_ok, 1)

            def edge_tile_hot(t):
                dve.wait_ge(iota_ok, 1)
                if t >= HOTS:
                    dve.wait_ge(hot_used, t - HOTS + 1)
                nc.vector.tensor_scalar(hot_src[:, t % HOTS, :], iota[:], cols[:, 0, t:t + 1], None,
                                        ALU.is_equal).then_inc(hot_ok, 1)
                if t % EG == 0:
                    dve.wait_ge(value_ok, t // EG + 1)
                nc.vector.tensor_scalar(hot_dst[:, t % HOTS, :], iota[:], cols[:, 1, t:t + 1],
                                        value_bits[:, t:t + 1].bitcast(F32), ALU.is_equal,
                                        ALU.mult).then_inc(hot_ok, 1)

            def edge_unit(g):
                edge_unit_later(g, tiles_of(g))
                edge_unit_values(g)
                for t in tiles_of(g):
                    edge_tile_hot(t)

            for t in range(NT):
                for b in range(2):
                    if t == 0:
                        dve.wait_ge((x_half_in, x_in[0])[b], 16)
                    elif b == 0:
                        dve.wait_ge(x_in[t], 16)
                    nc.vector.bn_stats(stats[:, t, b, :], x_sb[:, t, b * HALF:(b + 1) * HALF]).then_inc(stats_step, 1)
                    if t >= 1 and b == 0:
                        shift_part(t - 1)
                dve.wait_ge(stats_step, 2 * (t + 1))
                nc.vector.bn_aggr(mean_var[:, t, :], stats[:, t, :, :]).then_inc(stats_agg, 1)
                dve.wait_ge(stats_agg, t + 1)
                nc.vector.tensor_scalar(var_eps[:, t:t + 1], mean_var[:, t, 1:2], EPS, None, ALU.add).then_inc(var_ok, 1)
                if t != 1:
                    edge_unit_later(0, range(t // 2, t // 2 + 1))
            shift_part(NT - 1)
            h_last = x_sb[:, NT - 1, HALF:F]
            dve.wait_ge(shift_ok, NT)
            nc.vector.tensor_scalar(h_last, h_last, rstd[:, NT - 1:NT], shift[:, NT - 1:NT], ALU.mult,
                                    ALU.add).then_inc(h_step, 1)
            edge_unit_later(0, range(2, 3))
            dve.wait_ge(h_step, 1)
            nc.vector.tensor_scalar(h_last, h_last, 0.0, None, ALU.max).then_inc(h_last_ok, 1)
            edge_unit_later(0, range(3, EG))

            def softplus_in():
                dve.wait_ge(small_in, 32)
                nc.vector.tensor_scalar(sp[:, 0, :], ew[:], -1.0, None, ALU.mult).then_inc(sp_step, 1)
                nc.vector.tensor_scalar(sp[:, 4, :], ew[:], 0.0, None, ALU.max).then_inc(sp_step, 1)
                dve.wait_ge(sp_step, 1)
                nc.vector.tensor_tensor(sp[:, 1, :], sp[:, 0, :], ew[:], ALU.min).then_inc(sp_in, 1)

            def softplus_out():
                dve.wait_ge(sp_ln, 1)
                dve.wait_ge(sp_step, 2)
                nc.vector.tensor_tensor(sp[:, 0, :], sp[:, 3, :], sp[:, 4, :], ALU.add).then_inc(sp_step, 1)
                dve.wait_ge(sp_step, 3)
                nc.vector.tensor_scalar(sp[:, 1, :], sp[:, 0, :], 1.0 / SCALE, None, ALU.mult).then_inc(sp_ok, 1)

            def tile_lo_part(t):
                hi, lo, b, psum = tile_place(t)
                if t < 3 * KT:
                    dve.wait_ge(tile_hi, t + 1)
                    nc.vector.scalar_tensor_tensor(lo, psum[:, 0:N], bias[:, b:b + 1], hi.bitcast(F32),
                                                   op0=ALU.add, op1=ALU.subtract).then_inc(tile_lo, 1)
                    return
                pair, is_k = (t - 3 * KT) // 2, t % 2
                turn = pair % 2
                for h in range(2):
                    own, other = rows_of(h)
                    dve.wait_ge(tile_hi, tile_hi_count(t) - 1 + h)
                    hi = (q2, k2_hi)[is_k][own, turn, h, :].bitcast(F32)
                    lo = k2_lo[own, turn, h, :] if is_k else q2[other, turn, h, :]
                    mm = nc.vector.scalar_tensor_tensor(lo, psum[own, 0:N], bias[own, b:b + 1], hi, op0=ALU.add,
                                                        op1=ALU.subtract)
                    if is_k:
                        mm.then_inc(k2_step if h == 0 else k2_read, 1)
                if not is_k:
                    mm.then_inc(tile_lo, 1)

            def k2_other_half(pair):
                turn = pair % 2
                dve.wait_ge(k2_step, pair + 1)
                dve.wait_ge(k2_read, pair + 1)
                for part in (k2_hi, k2_lo):
                    for h in range(2):
                        own, other = rows_of(h)
                        last = nc.vector.tensor_copy(part[other, turn, h, :], part[own, turn, h, :].bitcast(F32))
                last.then_inc(tile_lo, 1)

            def pair_lo_part(pair):
                dve.wait_ge(head_hi, pair + 1)
                nc.vector.tensor_tensor(a_lo[:, pair, :], head_out, a_hi[:, pair, :].bitcast(F32),
                                        ALU.subtract).then_inc(head_lo, 1)

            def build_mask():
                dve.wait_ge(hot_used, ET)
                dve.wait_ge(diag_ok, NT)
                for t in range(NT):
                    nc.vector.tensor_tensor(winner[:, t, :], mask_bank[t][:, 0:N], diag[:, t, :],
                                            ALU.max).then_inc(mask_step, 1)
                dve.wait_ge(mask_step, NT)
                nc.vector.tensor_scalar(cls[:], winner[:].bitcast(I32), 23, 3, ALU.logical_shift_right,
                                        ALU.bitwise_and).then_inc(mask_step, 1)
                nc.vector.tensor_scalar(mask[:], winner[:], 0.0, LOW, ALU.is_equal, ALU.mult).then_inc(mask_step, 1)
                dve.wait_ge(sp_ok, 1)
                for c in range(4):
                    dve.wait_ge(mask_step, NT + 2 + 2 * c)
                    nc.vector.tensor_scalar(pick[:, c % 2], cls[:], float(c), sp[:, 1, c:c + 1], ALU.is_equal,
                                            ALU.mult).then_inc(mask_step, 1)
                    dve.wait_ge(mask_step, NT + 3 + 2 * c)
                    nc.vector.tensor_tensor(mask[:], mask[:], pick[:, c % 2], ALU.add).then_inc(
                        mask_step if c < 3 else mask_ok, 1)

            edge_unit_values(0)
            for k in range(KT):
                dve.wait_ge(h_hi, k + 1)
                nc.vector.tensor_tensor(a_lo[:, k, :], h_bank[k % 3][:, 0:N], a_hi[:, k, :].bitcast(F32),
                                        ALU.subtract).then_inc(h_lo, 1)
                if 0 <= k - HOT_FROM < EG:
                    edge_tile_hot(k - HOT_FROM)
            unit = 1
            for t in range(KT):
                for _ in range(UNITS_OF_SLAB[t]):
                    edge_unit(unit)
                    unit += 1
                tile_lo_part(t)
                if t == 1:
                    softplus_in()
                if t == 4:
                    softplus_out()
            build_mask()
            for g in range(GS):
                for t in range(NT):
                    dve.wait_ge(v2_hi, g * NT + t + 1)
                    pairs = slice(g * PAIRS // GS, (g + 1) * PAIRS // GS)
                    nc.vector.tensor_tensor(
                        v2[:, t, pairs, 1:3, :], v2_bank[g][t][:, :].rearrange("p (a b d) -> p a b d", b=2, d=D),
                        v2[:, t, pairs, 0:4:3, :].bitcast(F32), ALU.subtract).then_inc(v2_lo, 1)
            for first, hi, lo, b in ((KT, b_hi, b_lo, BQ), (2 * KT, c_hi, c_lo, BK)):
                with dve.Fori(0, KT - 1, 2) as pair_of_tiles:
                    for turn in range(2):
                        j = pair_of_tiles + turn
                        dve.wait_ge(tile_hi, first + 1 + j)
                        nc.vector.scalar_tensor_tensor(
                            lo[:, bass.ds(j, 1), :].rearrange("p j n -> p (j n)"), tile_bank[turn][:, 0:N],
                            bias[:, bass.ds(b + j, 1)],
                            hi[:, bass.ds(j, 1), :].rearrange("p j n -> p (j n)").bitcast(F32), op0=ALU.add,
                            op1=ALU.subtract).then_inc(tile_lo, 1)
            for t in range(3 * KT, 3 * KT + TILES_AHEAD):
                tile_lo_part(t)
                if t == 3 * KT + 1:
                    k2_other_half(0)

            def neg_max_part(i, t):
                dve.wait_ge(masked, i * NT + t + 1)
                nc.vector.tensor_scalar(neg_max[:, i % 2, t:t + 1], row_max[:, i % 2, t:t + 1], -SCALE, None,
                                        ALU.mult).then_inc(neg_max_ok, 1)

            def pt_lo_part(h, m):
                dve.wait_ge(pt_hi_ok, h * NT + m + 1)
                nc.vector.tensor_tensor(pt_lo[:, m, :], pt_bank[m][:, 0:N], pt_hi[:, m, :].bitcast(F32),
                                        ALU.subtract).then_inc(pt_lo_ok, 1)

            for i in range(H + 1):
                if i < H:
                    for t in range(NT):
                        dve.wait_ge(score_done, i * NT + t + 1)
                        if i == 0:
                            dve.wait_ge(mask_ok, 1)
                        nc.vector.tensor_tensor_reduce(
                            out=prob[:, i % 2, t, :], in0=score_bank[t][:, 0:N], in1=mask[:, t, :], scale=1.0,
                            scalar=-3.4e38, op0=ALU.add, op1=ALU.max,
                            accum_out=row_max[:, i % 2, t:t + 1]).then_inc(masked, 1)
                        if t >= 1:
                            neg_max_part(i, t - 1)
                    neg_max_part(i, NT - 1)
                if i >= 1:
                    for m in range(NT):
                        pt_lo_part(i - 1, m)
                if i == H - TILES_AHEAD:
                    k2_other_half(PAIRS - 1)
                if i < H:
                    for t in range(NT):
                        dve.wait_ge(exp_done, i * NT + t + 1)
                        nc.vector.reciprocal(row_inv[:, i % 2, t:t + 1], row_sum[:, i % 2, t:t + 1]).then_inc(inv_ok, 1)
                if H - TILES_AHEAD <= i < H:
                    for t in range(1, NT):
                        dve.wait_ge(inv_ok, i * NT + t + 1)
                        nc.vector.tensor_scalar(prob[:, i % 2, t, :], prob[:, i % 2, t, :],
                                                row_inv[:, i % 2, t:t + 1], None, ALU.mult).then_inc(prob_ok, 1)
                if i % 2 == 1 and i < H - TILES_AHEAD:
                    k2_other_half((i + 1) // 2)
                if i < H - TILES_AHEAD:
                    tile_lo_part(3 * KT + TILES_AHEAD + i)
                if i == H - 1:
                    pair_lo_part(PAIRS - 2)
                if i >= 1:
                    own, _ = rows_of(i - 1)
                    dve.wait_ge(half_ok, i)
                    if i >= 3:
                        dve.wait_ge(head_lo, (i - 1) // 2)
                    nc.vector.tensor_tensor(head_out[own, :], head_bank[own, 0:N], half_sum[own, :],
                                            ALU.add).then_inc(head_sum, 1)
            pair_lo_part(PAIRS - 1)
            dve.wait_ge(y_ok, NT)
            for i, (_, n, cols_out, psum) in enumerate(out_pieces):
                dve.wait_ge(out_done, i + 1)
                nc.vector.tensor_tensor(y[:, n, cols_out], psum, y[:, n, cols_out], ALU.add).then_inc(out_ok, 1)

        @block.tensor
        def _(pe):
            def products(psum, w, a, first, last, h_tiles=0):
                if h_tiles:
                    pe.wait_ge(h_hi, h_tiles)
                nc.tensor.matmul(psum, w[0], a[0], start=first, stop=False)
                nc.tensor.matmul(psum, w[1], a[0], start=False, stop=False)
                if h_tiles:
                    pe.wait_ge(h_lo, h_tiles)
                return nc.tensor.matmul(psum, w[0], a[1], start=False, stop=last)

            def keys(g):
                for t in tiles_of(g):
                    mm = nc.tensor.matmul(key_bank[g % 2][:, (t % EG) * P:(t % EG + 1) * P],
                                          select[:, t:t + 1].to_broadcast([P, P]), rows[:], start=True, stop=True)
                mm.then_inc(keys_done, 1)

            def edge_unit(g):
                for t in tiles_of(g):
                    pe.wait_ge(hot_ok, 2 * (t + 1))
                    for n in range(NT):
                        mm = nc.tensor.matmul(mask_bank[n][:, 0:N], hot_src[:, t % HOTS, n * P:(n + 1) * P],
                                              hot_dst[:, t % HOTS, :], start=(t == 0), stop=(t == ET - 1))
                    mm.then_inc(hot_used, 1)
                if g + 2 < GROUPS:
                    pe.wait_ge(later_ok, tiles_of(g)[-1] + 1)
                    keys(g + 2)

            def split_slab(s):
                pe.wait_ge(slab_lo, s + 1)
                return split_place(s)

            def tile(t, a_h, a_l, ks=range(KT)):
                if t == 0 and ks[-1] < KT // 2:
                    pe.wait_ge(half_lo, 1)
                    hi, lo = split_place(0)
                else:
                    hi, lo = split_slab(slab_of(t))
                if t >= 3 * KT + 5:
                    if t % 2 == 0:
                        pe.wait_ge(k2_read, t // 2 - 3 * KT // 2)
                    else:
                        pe.wait_ge(tile_lo, t)
                elif t >= 2:
                    pe.wait_ge(tile_lo, t - 1)
                psum = tile_place(t)[3]
                for k in ks:
                    c = slice(k * P, (k + 1) * P)
                    mm = products(psum[:, 0:N], (hi[:, c], lo[:, c]), (a_h[:, k, :], a_l[:, k, :]), k == 0,
                                  k == KT - 1, k + 1 if t == 0 else 0)
                if k == KT - 1:
                    mm.then_inc(slab_used, 1)

            def moving(s, base, a_h, a_l, banks, done):
                hi, lo = split_slab(s)
                g, part = (s - base) // KS, (s - base) % KS
                for n in range(NT):
                    m = slice(n * P, (n + 1) * P)
                    for b in range(GS):
                        k, c = part * GS + b, slice(b * HALF, (b + 1) * HALF)
                        mm = products(banks[g][n][:, :], (a_h[:, k, m], a_l[:, k, m]), (hi[:, c], lo[:, c]),
                                      k == 0, k == KT - 1)
                    if n == NT - 1:
                        mm.then_inc(slab_used, 1)
                    elif part == KS - 1:
                        mm.then_inc(done, 1)

            pe.wait_ge(rows_ok, 1)
            pe.wait_ge(select_ok, 1)
            keys(0)
            pe.wait_ge(shift_ok, 1)
            pe.wait_ge(iota_ok, 1)
            for _ in range(WARM):
                nc.tensor.matmul(tile_bank[0][:, 0:N], select[:, 0:1].to_broadcast([P, P]), iota[:], start=True, stop=True)
            pe.wait_ge(h_ok, NT)
            pe.wait_ge(ident_ok, 1)
            for k in range(KT):
                if k == HALF // P:
                    pe.wait_ge(h_last_ok, 1)
                if k >= 3:
                    pe.wait_ge(h_lo, k - 2)
                for t in range(NT):
                    mm = nc.tensor.transpose(h_bank[k % 3][:, t * P:(t + 1) * P], x_sb[:, t, k * P:(k + 1) * P], ident[:])
                mm.then_inc(h_turned, 1)
                if k >= 2:
                    tile(0, a_hi, a_lo, [k - 2])
            pe.wait_ge(h_lo, KT - 2)
            keys(1)
            edge_unit(0)
            tile(0, a_hi, a_lo, range(KT - 2, KT))
            unit = 1
            for t in range(KT):
                if t >= 1:
                    tile(t, a_hi, a_lo)
                for _ in range(UNITS_OF_SLAB[t]):
                    edge_unit(unit)
                    unit += 1
            for s in range(VV0, Q0):
                if s == VV0 + KS:
                    pe.wait_ge(mask_step, NT)
                if s - VV0 < KS:
                    pe.wait_ge(tile_lo, (s - VV0 + 1) * GS)
                moving(s, VV0, b_hi, b_lo, v2_bank, v2_done)
            for t in range(KT, 3 * KT):
                tile(t, a_hi, a_lo)

            def pair_tile(t):
                if t % 2 == 0:
                    tile(t, b_hi, b_lo)
                else:
                    tile(t, c_hi, c_lo)

            def scores(h):
                turn = h // 2 % 2
                if h % 2 == 0:
                    pe.wait_ge(tile_lo, 3 * KT + h + 2)
                for n in range(NT):
                    if h >= 1:
                        pe.wait_ge(masked, (h - 1) * NT + n + 1)
                    m = slice(n * P, (n + 1) * P)
                    nc.tensor.matmul(score_bank[n][:, 0:N], q2[:, turn, h % 2, m], k2_hi[:, turn, h % 2, :],
                                     start=True, stop=False)
                    nc.tensor.matmul(score_bank[n][:, 0:N], q2[:, turn, h % 2, m], k2_lo[:, turn, h % 2, :],
                                     start=False, stop=True).then_inc(score_done, 1)

            def turn_probs(h):
                pe.wait_ge(prob_ok, (h + 1) * NT)
                for m in range(NT):
                    if h >= 1:
                        pe.wait_ge(pt_lo_ok, (h - 1) * NT + m + 1)
                    for n in range(NT):
                        mm = nc.tensor.transpose(pt_bank[m][:, n * P:(n + 1) * P],
                                                 prob[:, h % 2, n, m * P:(m + 1) * P], ident[:])
                    mm.then_inc(pt_done, 1)

            def heads_values(h):
                pair = h // 2
                if h >= 1:
                    pe.wait_ge(head_sum, h)
                else:
                    pe.wait_ge(k2_read, 2)
                for m in range(NT):
                    pe.wait_ge(pt_lo_ok, h * NT + m + 1)
                    w = v2[:, m, pair, 2 * (h % 2):2 * (h % 2) + 2, :]
                    nc.tensor.matmul(head_bank[:, 0:N], w, pt_hi[:, m, :], start=(m == 0), stop=False)
                    mm = nc.tensor.matmul(head_bank[:, 0:N], w, pt_lo[:, m, :], start=False, stop=(m == NT - 1))
                mm.then_inc(head_done, 1)

            def out_part(piece, ks):
                g, n, cols_out, psum = out_pieces[piece]
                m = slice(n * P, (n + 1) * P)
                for k in ks:
                    s, b = O0 + g * KS + k // GS, k % GS
                    pe.wait_ge(head_lo, k + 1)
                    hi, lo = split_slab(s)
                    start = b * HALF - g * HALF
                    c = slice(cols_out.start + start, cols_out.stop + start)
                    mm = products(psum, (a_hi[:, k, m], a_lo[:, k, m]), (hi[:, c], lo[:, c]),
                                  k == 0, k == KT - 1)
                if k == KT - 1:
                    mm.then_inc(out_done, 1)

            pe.wait_ge(v2_lo, GS * NT)
            for t in range(TILES_AHEAD):
                pair_tile(3 * KT + t)
            for i in range(H + 1):
                if i < H:
                    scores(i)
                if i == H:
                    out_part(2, range(0, KT - 2))
                if i >= 1:
                    turn_probs(i - 1)
                if i < H - TILES_AHEAD:
                    pair_tile(3 * KT + TILES_AHEAD + i)
                elif i == H - 3:
                    pe.wait_ge(k2_read, PAIRS)
                    out_part(0, range(0, KT // 2))
                elif i == H - 2:
                    out_part(0, range(KT // 2, KT - 2))
                elif i == H - 1:
                    pe.wait_ge(masked, (H - 1) * NT + 1)
                    out_part(1, range(0, KT - 2))
                else:
                    for n in range(NT):
                        out_part(n, [KT - 2])
                if i >= 1:
                    heads_values(i - 1)
            out_part(NT, range(0, KT - 1))
            for n in range(NT):
                out_part(n, [KT - 1])
            out_part(NT, [KT - 1])
            out_part(NT + 1, range(KT))
            out_part(NT + 2, range(KT))
            out_part(NT + 3, range(KT))


def kernel(x, src, dst, edge_type_5, L0_gnn_edge_type_weights, L0_gnn_wq, L0_gnn_bq, L0_gnn_wk, L0_gnn_bk,
           L0_gnn_wv, L0_gnn_bv, L0_gnn_wiq, L0_gnn_biq, L0_gnn_wik, L0_gnn_bik, L0_gnn_wiv, L0_gnn_biv,
           L0_gnn_wo, L0_gnn_bo):
    import concourse.bacc as bacc
    from concourse.bass_utils import run_bass_kernel_spmd

    def stay(w):
        return np.asarray(w).reshape(KT, P, KT, P).transpose(0, 3, 2, 1).reshape(KT, P, F)

    def move(w):
        return np.asarray(w).reshape(GS, HALF, KS, GS, P).transpose(0, 2, 4, 3, 1).reshape(KT, P, F)

    second = np.stack([stay(L0_gnn_wiq), stay(L0_gnn_wik)], axis=1).reshape(2 * KT, P, F)
    slabs = np.concatenate([stay(L0_gnn_wv), move(L0_gnn_wiv), stay(L0_gnn_wq), stay(L0_gnn_wk), second,
                            move(L0_gnn_wo)])
    edges = [np.asarray(a).reshape(ET, P) for a in (src, dst, edge_type_5)]
    rows = np.zeros((P, P), edges[0].dtype)
    rows[0:ET], rows[DST_ROW:DST_ROW + ET] = edges[0], edges[1]
    biases = np.concatenate([np.asarray(b).reshape(KT, P) for b in (
        L0_gnn_bq, L0_gnn_bk, L0_gnn_bv, L0_gnn_biq, L0_gnn_bik, L0_gnn_biv)]).T
    arrays = {
        "in_slabs": slabs, "in_x": np.asarray(x), "in_edge_cols": np.stack(edges).transpose(2, 0, 1),
        "in_edge_rows": rows, "in_edge_weights": np.asarray(L0_gnn_edge_type_weights), "in_biases": biases,
        "in_bo": np.asarray(L0_gnn_bo),
    }
    arrays = {name: np.ascontiguousarray(a) for name, a in arrays.items()}
    nc = bacc.Bacc("TRN2", target_bir_lowering=False, num_devices=1)
    args = [nc.dram_tensor(name, a.shape, mybir.dt.from_np(a.dtype), kind="ExternalInput").ap()
            for name, a in arrays.items()]
    out = nc.dram_tensor("out_y", (N, F), F32, kind="ExternalOutput").ap()
    gat_kernel(nc, *args, out)
    return run_bass_kernel_spmd(nc, [arrays], core_ids=[0]).results[0]["out_y"]
```
